# Optimizing a Trainium2 kernel written in Bass

```python
import numpy as np
import jax
import jax.numpy as jnp

def _softmax(x, axis=-1):
    return jax.nn.softmax(x, axis=axis)

def _gelu(x):
    return jax.nn.gelu(x, approximate=True)

def _silu(x):
    return jax.nn.silu(x)

def _sigmoid(x):
    return jax.nn.sigmoid(x)

def _layernorm(x, axis=-1, eps=1e-05):
    m = jnp.mean(x, axis=axis, keepdims=True)
    v = jnp.var(x, axis=axis, keepdims=True)
    return (x - m) / jnp.sqrt(v + eps)

def _scatter_add(tgt, idx, src, axis=0):
    return tgt.at[idx].add(src)

def _segment_sum(src, seg, n):
    return jax.ops.segment_sum(src, seg, n)
kernel_name = 'mk_vit_tower_d1_tok_img256_r4_e35d66'

def setup_inputs(seed: int=0):
    np.random.seed(seed)
    _w = jnp.asarray

    def _rec_inputs():
        import jax
        import jax.numpy as jnp
        _rk = jax.random.key(seed)
        x = -0.000125008 + 0.999885 * jax.random.normal(jax.random.fold_in(_rk, 1), (64, 64, 64, 64), jnp.float32)
        return x
    x = _rec_inputs()

    def _L0_tok_setup():
        import jax, jax.numpy as jnp
        import numpy as np
        B, C, H, W = (32, 64, 64, 64)
        STRIDE, HEADS = (4, 8)

        def _ln(x, w, b):
            mu = x.mean(-1, keepdims=True)
            var = ((x - mu) ** 2).mean(-1, keepdims=True)
            return (x - mu) * jax.lax.rsqrt(var + 1e-05) * w + b
        key = jax.random.key(seed)
        ks = jax.random.split(key, 4)
        return {'features': jax.random.normal(ks[0], (B, C, H, W), dtype=jnp.float32), 'ln_q_w': jnp.ones((C,), jnp.float32), 'ln_q_b': jnp.zeros((C,), jnp.float32), 'Wq': jax.random.normal(ks[1], (C, C), dtype=jnp.float32) * 0.02, 'ln_kv_w': jnp.ones((C,), jnp.float32), 'ln_kv_b': jnp.zeros((C,), jnp.float32), 'Wkv': jax.random.normal(ks[2], (2 * C, C), dtype=jnp.float32) * 0.02, 'proj_w': jax.random.normal(ks[3], (C, C), dtype=jnp.float32) * 0.02, 'proj_b': jnp.zeros((C,), jnp.float32), 'conv_stride': STRIDE, 'num_heads': HEADS}
    _L0_tok_all = _L0_tok_setup()
    _L0_tok_in = {k: v for k, v in _L0_tok_all.items() if k in ('ln_q_w', 'ln_q_b', 'Wq', 'ln_kv_w', 'ln_kv_b', 'Wkv', 'proj_w', 'proj_b')}
    del _L0_tok_all

    def _L0_attn_setup():
        import jax, jax.numpy as jnp
        import numpy as np
        import math
        B, L = (4, 225)
        D_MODEL, D_STATE, D_INNER, DT_RANK = (64, 16, 128, 16)

        def _selective_scan(u, delta, A, Bm, Cm, D):
            dA = jnp.exp(jnp.einsum('bld,dn->lbdn', delta, A))
            dBu = jnp.einsum('bld,bln->lbdn', delta * u, Bm)
            Ct = jnp.transpose(Cm, (1, 0, 2))

            def step(h, inp):
                dA_t, dBu_t, c = inp
                h = dA_t * h + dBu_t
                return (h, jnp.einsum('bdn,bn->bd', h, c))
            h0 = jnp.zeros((u.shape[0], u.shape[2], A.shape[1]), u.dtype)
            _, ys = jax.lax.scan(step, h0, (dA, dBu, Ct))
            return jnp.transpose(ys, (1, 0, 2)) + D * u
        key = jax.random.key(seed)
        ks = jax.random.split(key, 10)
        nrm = lambda k, shape, s: jax.random.normal(k, shape, jnp.float32) * s
        hidden_states = jax.random.normal(ks[0], (B, L, D_MODEL), jnp.float32)
        W_in = nrm(ks[1], (2 * D_INNER, D_MODEL), D_MODEL ** (-0.5))
        W_xproj = nrm(ks[2], (DT_RANK + 2 * D_STATE, D_INNER), D_INNER ** (-0.5))
        s = DT_RANK ** (-0.5)
        W_dt = jax.random.uniform(ks[3], (D_INNER, DT_RANK), jnp.float32, -s, s)
        dt = jnp.exp(jax.random.uniform(ks[4], (D_INNER,), jnp.float32) * (math.log(0.1) - math.log(0.001)) + math.log(0.001))
        b_dt = dt + jnp.log(-jnp.expm1(-dt))
        A_log = jnp.broadcast_to(jnp.log(jnp.arange(1, D_STATE + 1, dtype=jnp.float32)), (D_INNER, D_STATE))
        W_global = nrm(ks[5], (2 * D_INNER, 2 * D_INNER), (2 * D_INNER) ** (-0.5))
        W_gate = nrm(ks[6], (2 * D_INNER, 2 * D_INNER), (2 * D_INNER) ** (-0.5))
        W_out = nrm(ks[7], (D_MODEL, 2 * D_INNER), (2 * D_INNER) ** (-0.5))
        return {'hidden_states': hidden_states, 'W_in': W_in, 'W_xproj': W_xproj, 'W_dt': W_dt, 'b_dt': b_dt, 'A_log_f': jnp.array(A_log), 'A_log_b': jnp.array(A_log), 'D_f': jnp.ones(D_INNER, jnp.float32), 'D_b': jnp.ones(D_INNER, jnp.float32), 'W_global': W_global, 'b_global': jnp.zeros(2 * D_INNER, jnp.float32), 'W_gate': W_gate, 'b_gate': jnp.zeros(2 * D_INNER, jnp.float32), 'W_out': W_out}
    _L0_attn_all = _L0_attn_setup()
    _L0_attn_in = {k: v for k, v in _L0_attn_all.items() if k in ('W_in', 'W_xproj', 'W_dt', 'b_dt', 'A_log_f', 'A_log_b', 'D_f', 'D_b', 'W_global', 'b_global', 'W_gate', 'b_gate', 'W_out')}
    del _L0_attn_all

    def _L0_ffn_setup():
        import jax, jax.numpy as jnp
        import numpy as np
        DIM = 64
        HEADS = 8
        NUM_KEYS = 64
        NUM_KV = NUM_KEYS ** 2
        PK_TOPK = 16
        FINAL_TOPK = 16
        DIM_KEY = DIM // 2
        P = 2

        def _pk(x, Wq_pk, pk_keys):
            b, n, _ = x.shape
            q = (x @ Wq_pk).reshape(b, n, P, HEADS, DIM_KEY).transpose(2, 0, 1, 3, 4)
            sim = jnp.einsum('pbnhd,pkhd->pbnhk', q, pk_keys)
            scores, idx = jax.lax.top_k(sim, PK_TOPK)
            idx0 = idx[0]
            idx1 = idx[1] * NUM_KEYS
            index = (idx0[..., :, None] + idx1[..., None, :]).reshape(b, n, HEADS, PK_TOPK * PK_TOPK)
            score = (scores[0][..., :, None] + scores[1][..., None, :]).reshape(b, n, HEADS, PK_TOPK * PK_TOPK)
            final_scores, pk_idx = jax.lax.top_k(score, FINAL_TOPK)
            final_indices = jnp.take_along_axis(index, pk_idx, axis=-1)
            final_scores = jax.nn.softmax(final_scores, axis=-1)
            return (final_scores, final_indices)
        key = jax.random.key(seed)
        ks = jax.random.split(key, 7)
        b, n = (2, 256)
        std = 0.02
        x = jax.random.normal(ks[0], (b, n, DIM), dtype=jnp.float32)
        Wq_pk = jax.random.normal(ks[1], (DIM, P * HEADS * DIM_KEY), dtype=jnp.float32) * std
        pk_keys = jax.random.normal(ks[2], (P, NUM_KEYS, HEADS, DIM_KEY), dtype=jnp.float32) * std
        Wq = jax.random.normal(ks[3], (DIM, HEADS * DIM), dtype=jnp.float32) * std
        keys_table = jax.random.normal(ks[4], (NUM_KV * HEADS, DIM), dtype=jnp.float32) * std
        values_table = jax.random.normal(ks[5], (NUM_KV * HEADS, DIM), dtype=jnp.float32) * std
        Wo = jax.random.normal(ks[6], (DIM * HEADS, DIM), dtype=jnp.float32) * std
        return {'x': x, 'Wq_pk': Wq_pk, 'pk_keys': pk_keys, 'Wq': Wq, 'keys_table': keys_table, 'values_table': values_table, 'Wo': Wo}
    _L0_ffn_all = _L0_ffn_setup()
    _L0_ffn_in = {k: v for k, v in _L0_ffn_all.items() if k in ('Wq_pk', 'pk_keys', 'Wq', 'keys_table', 'values_table', 'Wo')}
    del _L0_ffn_all
    return {'x': x, 'L0_tok_ln_q_w': _L0_tok_in['ln_q_w'], 'L0_tok_ln_q_b': _L0_tok_in['ln_q_b'], 'L0_tok_Wq': _L0_tok_in['Wq'], 'L0_tok_ln_kv_w': _L0_tok_in['ln_kv_w'], 'L0_tok_ln_kv_b': _L0_tok_in['ln_kv_b'], 'L0_tok_Wkv': _L0_tok_in['Wkv'], 'L0_tok_proj_w': _L0_tok_in['proj_w'], 'L0_tok_proj_b': _L0_tok_in['proj_b'], 'L0_attn_W_in': _L0_attn_in['W_in'], 'L0_attn_W_xproj': _L0_attn_in['W_xproj'], 'L0_attn_W_dt': _L0_attn_in['W_dt'], 'L0_attn_b_dt': _L0_attn_in['b_dt'], 'L0_attn_A_log_f': _L0_attn_in['A_log_f'], 'L0_attn_A_log_b': _L0_attn_in['A_log_b'], 'L0_attn_D_f': _L0_attn_in['D_f'], 'L0_attn_D_b': _L0_attn_in['D_b'], 'L0_attn_W_global': _L0_attn_in['W_global'], 'L0_attn_b_global': _L0_attn_in['b_global'], 'L0_attn_W_gate': _L0_attn_in['W_gate'], 'L0_attn_b_gate': _L0_attn_in['b_gate'], 'L0_attn_W_out': _L0_attn_in['W_out'], 'L0_ffn_Wq_pk': _L0_ffn_in['Wq_pk'], 'L0_ffn_pk_keys': _L0_ffn_in['pk_keys'], 'L0_ffn_Wq': _L0_ffn_in['Wq'], 'L0_ffn_keys_table': _L0_ffn_in['keys_table'], 'L0_ffn_values_table': _L0_ffn_in['values_table'], 'L0_ffn_Wo': _L0_ffn_in['Wo']}

def reference(x, L0_tok_ln_q_w, L0_tok_ln_q_b, L0_tok_Wq, L0_tok_ln_kv_w, L0_tok_ln_kv_b, L0_tok_Wkv, L0_tok_proj_w, L0_tok_proj_b, L0_attn_W_in, L0_attn_W_xproj, L0_attn_W_dt, L0_attn_b_dt, L0_attn_A_log_f, L0_attn_A_log_b, L0_attn_D_f, L0_attn_D_b, L0_attn_W_global, L0_attn_b_global, L0_attn_W_gate, L0_attn_b_gate, L0_attn_W_out, L0_ffn_Wq_pk, L0_ffn_pk_keys, L0_ffn_Wq, L0_ffn_keys_table, L0_ffn_values_table, L0_ffn_Wo):
    import jax
    import jax.numpy as jnp

    def _L0_tok_ref(features, ln_q_w, ln_q_b, Wq, ln_kv_w, ln_kv_b, Wkv, proj_w, proj_b, conv_stride, num_heads):
        import jax, jax.numpy as jnp
        import numpy as np
        B, C, H, W = (32, 64, 64, 64)
        STRIDE, HEADS = (4, 8)

        def _ln(x, w, b):
            mu = x.mean(-1, keepdims=True)
            var = ((x - mu) ** 2).mean(-1, keepdims=True)
            return (x - mu) * jax.lax.rsqrt(var + 1e-05) * w + b
        s = conv_stride
        b, c, hh, ww = features.shape
        h, w = (hh // s, ww // s)
        hw, n, d = (h * w, s * s, c // num_heads)
        scale = c ** (-0.5)
        x = features.reshape(b, c, h, s, w, s)
        reduce_feats = x.mean((3, 5)).reshape(b, c, hw).transpose(0, 2, 1)
        unf = x.transpose(0, 1, 2, 4, 3, 5).reshape(b, c, hw, n).transpose(0, 2, 3, 1)
        q = _ln(reduce_feats, ln_q_w, ln_q_b) @ Wq.T
        q = q.reshape(b, hw, num_heads, d).transpose(0, 2, 1, 3)
        kv = _ln(unf, ln_kv_w, ln_kv_b) @ Wkv.T
        kv = kv.reshape(b, hw, n, 2, num_heads, d).transpose(3, 0, 4, 1, 2, 5)
        k, v = (kv[0], kv[1])
        attn = jax.nn.softmax(jnp.einsum('bhpd,bhpnd->bhpn', q * scale, k), axis=-1)
        aggre = jnp.einsum('bhpn,bhpnd->bhpd', attn, v)
        aggre = aggre.transpose(0, 2, 1, 3).reshape(b, hw, c)
        return reduce_feats + aggre @ proj_w.T + proj_b

    def _L0_attn_ref(hidden_states, W_in, W_xproj, W_dt, b_dt, A_log_f, A_log_b, D_f, D_b, W_global, b_global, W_gate, b_gate, W_out):
        import jax, jax.numpy as jnp
        import numpy as np
        import math
        B, L = (4, 225)
        D_MODEL, D_STATE, D_INNER, DT_RANK = (64, 16, 128, 16)

        def _selective_scan(u, delta, A, Bm, Cm, D):
            dA = jnp.exp(jnp.einsum('bld,dn->lbdn', delta, A))
            dBu = jnp.einsum('bld,bln->lbdn', delta * u, Bm)
            Ct = jnp.transpose(Cm, (1, 0, 2))

            def step(h, inp):
                dA_t, dBu_t, c = inp
                h = dA_t * h + dBu_t
                return (h, jnp.einsum('bdn,bn->bd', h, c))
            h0 = jnp.zeros((u.shape[0], u.shape[2], A.shape[1]), u.dtype)
            _, ys = jax.lax.scan(step, h0, (dA, dBu, Ct))
            return jnp.transpose(ys, (1, 0, 2)) + D * u
        silu = lambda t: t * jax.nn.sigmoid(t)
        xz = hidden_states @ W_in.T
        x, z = jnp.split(xz, 2, axis=-1)
        x = silu(x)
        x_dbl = x @ W_xproj.T
        dt_r = x_dbl[..., :DT_RANK]
        Bm = x_dbl[..., DT_RANK:DT_RANK + D_STATE]
        Cm = x_dbl[..., DT_RANK + D_STATE:]
        dt = jax.nn.softplus(dt_r @ W_dt.T + b_dt)
        A_f = -jnp.exp(A_log_f)
        A_b = -jnp.exp(A_log_b)
        flip = lambda t: t[:, ::-1]
        y_f = _selective_scan(x, dt, A_f, Bm, Cm, D_f)
        y_b = flip(_selective_scan(flip(x), flip(dt), A_b, flip(Bm), flip(Cm), D_b))
        zg = silu(z)
        y = jnp.concatenate([y_f * zg, y_b * zg], axis=-1)
        g = jax.nn.sigmoid((y.mean(axis=1) @ W_global.T + b_global) @ W_gate.T + b_gate)
        y = y * g[:, None, :]
        return y @ W_out.T

    def _L0_ffn_ref(x, Wq_pk, pk_keys, Wq, keys_table, values_table, Wo):
        import jax, jax.numpy as jnp
        import numpy as np
        DIM = 64
        HEADS = 8
        NUM_KEYS = 64
        NUM_KV = NUM_KEYS ** 2
        PK_TOPK = 16
        FINAL_TOPK = 16
        DIM_KEY = DIM // 2
        P = 2

        def _pk(x, Wq_pk, pk_keys):
            b, n, _ = x.shape
            q = (x @ Wq_pk).reshape(b, n, P, HEADS, DIM_KEY).transpose(2, 0, 1, 3, 4)
            sim = jnp.einsum('pbnhd,pkhd->pbnhk', q, pk_keys)
            scores, idx = jax.lax.top_k(sim, PK_TOPK)
            idx0 = idx[0]
            idx1 = idx[1] * NUM_KEYS
            index = (idx0[..., :, None] + idx1[..., None, :]).reshape(b, n, HEADS, PK_TOPK * PK_TOPK)
            score = (scores[0][..., :, None] + scores[1][..., None, :]).reshape(b, n, HEADS, PK_TOPK * PK_TOPK)
            final_scores, pk_idx = jax.lax.top_k(score, FINAL_TOPK)
            final_indices = jnp.take_along_axis(index, pk_idx, axis=-1)
            final_scores = jax.nn.softmax(final_scores, axis=-1)
            return (final_scores, final_indices)
        b, n, d = x.shape
        q = (x @ Wq).reshape(b, n, HEADS, DIM) * DIM ** (-0.5)
        kv_scores, indices = _pk(x, Wq_pk, pk_keys)
        offsets = jnp.arange(HEADS, dtype=indices.dtype) * NUM_KV
        ind = indices + offsets[None, None, :, None]
        k = jnp.einsum('bnhk,bnhkd->bnhd', kv_scores, keys_table[ind])
        v = jnp.einsum('bnhk,bnhkd->bnhd', kv_scores, values_table[ind])
        sim = jnp.einsum('bihd,bjhd->bhij', q, k)
        neg = -jnp.finfo(sim.dtype).max
        causal = jnp.tril(jnp.ones((n, n), dtype=bool))
        sim = jnp.where(causal, sim, neg)
        attn = jax.nn.softmax(sim, axis=-1)
        out = jnp.einsum('bhij,bjhd->bhid', attn, v)
        out = out.transpose(0, 2, 1, 3).reshape(b, n, HEADS * DIM)
        return out @ Wo
    h = _L0_tok_ref(x, L0_tok_ln_q_w, L0_tok_ln_q_b, L0_tok_Wq, L0_tok_ln_kv_w, L0_tok_ln_kv_b, L0_tok_Wkv, L0_tok_proj_w, L0_tok_proj_b, 4, 8)
    h = h + _L0_attn_ref(_layernorm(h, axis=-1), L0_attn_W_in, L0_attn_W_xproj, L0_attn_W_dt, L0_attn_b_dt, L0_attn_A_log_f, L0_attn_A_log_b, L0_attn_D_f, L0_attn_D_b, L0_attn_W_global, L0_attn_b_global, L0_attn_W_gate, L0_attn_b_gate, L0_attn_W_out)
    h = h + _L0_ffn_ref(_layernorm(h, axis=-1), L0_ffn_Wq_pk, L0_ffn_pk_keys, L0_ffn_Wq, L0_ffn_keys_table, L0_ffn_values_table, L0_ffn_Wo)
    return h

_drawn_inputs = setup_inputs


def setup_inputs(seed=0):
    import zlib

    import numpy as np

    out = dict(_drawn_inputs(seed))
    spreads = {'L0_tok_ln_q_w': (1.0, 0.6),
     'L0_tok_ln_q_b': (0.0, 2.0),
     'L0_tok_ln_kv_w': (1.0, 0.6),
     'L0_tok_ln_kv_b': (0.0, 0.612),
     'L0_tok_proj_b': (0.0, 0.1),
     'L0_attn_D_f': (1.0, 0.2),
     'L0_attn_D_b': (1.0, 0.2),
     'L0_attn_b_global': (0.0, 0.336),
     'L0_attn_b_gate': (0.0, 0.312)}
    factors = {'L0_tok_Wq': 42.232,
     'L0_attn_W_dt': 3.538,
     'L0_attn_W_global': 2.782,
     'L0_ffn_Wq_pk': 8.0,
     'L0_ffn_pk_keys': 8.0,
     'L0_ffn_Wq': 64.0,
     'L0_ffn_keys_table': 64.0,
     'L0_ffn_values_table': 8.0,
     'L0_ffn_Wo': 8.0}
    for name, (base, spread) in spreads.items():
        noise = np.random.default_rng([zlib.crc32(name.encode()), seed]).standard_normal(out[name].shape)
        drawn = base * np.exp(spread * noise) if base else spread * noise
        out[name] = jnp.asarray(drawn.astype(out[name].dtype))
    for name, factor in factors.items():
        out[name] = (out[name] * factor).astype(out[name].dtype)
    return out
```

```python
from contextlib import ExitStack

import numpy as np
import concourse.bass as bass
from concourse import mybir

ALU = mybir.AluOpType
ACT = mybir.ActivationFunctionType
AX = mybir.AxisListType.X
F32 = mybir.dt.float32
U32 = mybir.dt.uint32

P = 128
IMAGES = 64
C = 64
SIDE = 16
TOK = SIDE * SIDE
TILES = TOK // P
N = 16
HEADS = 8
D = C // HEADS
INNER = 128
STATE = 16
RANK = 16
PK_HEADS = 8
KEYS = 64
TOPK = 16
EPS = 1e-5
KVW = 2 * C + 2
UNITS = PK_HEADS * TILES
SLOTS = 8
SCRATCH = 3200

STAIRS = []
_pos = 0
_r = 0
while _r < TOPK:
    _c = TOPK // (_r + 1)
    _rows = 1
    while _r + _rows < TOPK and TOPK // (_r + _rows + 1) == _c:
        _rows += 1
    STAIRS.append((_r, _rows, _c, _pos))
    _pos += _rows * _c
    _r += _rows
PAIRS = _pos
FRAC = 1.0 / 16384.0

KV_CHUNKS = [(n, min(3, N - n)) for n in range(0, N, 3)]
NKV = TILES * len(KV_CHUNKS)
NBC = STATE // 2


def host_constants():
    ident = np.eye(P, dtype=np.float32)
    i = np.arange(P)
    causal = np.where(i[None, :] <= i[:, None], 0.0, -1e30).astype(np.float32)
    pos = np.tile(np.arange(PAIRS, dtype=np.float32), (P, 1))
    head = np.repeat(np.arange(UNITS) // TILES * KEYS * KEYS, TOPK).astype(np.float32)
    return ident, causal, np.ascontiguousarray(pos), np.tile(head, (P, 1))


def build(nc, x, wkvT, lnkv, wqT, lnq, projE, w_inT, w_x, w_xT, w_dtT, b_dt, a_log, d_skip,
          w_global, w_gateT, b_global, b_gate, w_outT, wq_pkT, pk_keysT, w_q, w_o, table,
          ident_d, causal_d, pos_d, headoff_d, out):
    with ExitStack() as ctx:
        def sb(name, shape, dt=F32):
            return ctx.enter_context(nc.sbuf_tensor(name, shape, dt))

        def sem(name):
            return ctx.enter_context(nc.semaphore(name))

        bank = [ctx.enter_context(nc.psum_tensor(f"bank{i}", [P, 512], F32)) for i in range(8)]
        big_ps = bank[0:2]
        small_ps = bank[2]
        turn_ps = bank[3]
        scan_ps = bank[4]
        sum_ps = bank[5]
        score_ps = bank[6]
        prob_ps = bank[7]

        gath = sb("gath", [P, SLOTS, TOPK, 2 * C])
        spare = gath[:].rearrange("p s j c -> p (s j c)")
        wglob = spare[:, 0:1024 // 2].rearrange("p (k m) -> p k m", k=2)
        wgate = spare[:, 512:1024].rearrange("p (k m) -> p k m", k=2)
        wqpk = spare[0:32, 1024:2048]
        pkk = spare[0:32, 2048:3072]

        ident = sb("ident", [P, P])
        causal = sb("causal", [P, P])
        pos = sb("pos", [P, PAIRS])
        headoff = sb("headoff", [P, UNITS * TOPK])
        wkv_raw = sb("wkv_raw", [C, 2 * C])
        lnkv_s = sb("lnkv_s", [C, 2])
        wq_raw = sb("wq_raw", [C, C])
        lnq_s = sb("lnq_s", [C, 2])
        proj_raw = sb("proj_raw", [C + 1, C])
        w_in = sb("w_in", [C, 2 * INNER])
        wx_rows = sb("wx_rows", [RANK, INNER])
        wx_cols = sb("wx_cols", [INNER, RANK + 2 * STATE])
        wdt = sb("wdt", [RANK, INNER])
        bdt = sb("bdt", [INNER, 1])
        alog = sb("alog", [INNER, 2 * STATE])
        dskip = sb("dskip", [INNER, 2])
        bglob = sb("bglob", [P, 2])
        bgate = sb("bgate", [P, 2])
        wout = sb("wout", [P, 2, C])
        wq_ffn = sb("wq_ffn", [C, PK_HEADS * C])
        wo_ffn = sb("wo_ffn", [P, PK_HEADS, C])
        wkv = sb("wkv", [P, KVW])
        mean16 = sb("mean16", [C, C])
        ones64 = sb("ones64", [C, C])
        lq = sb("lq", [C, C + 1])
        wq = sb("wq", [C + 1, C + HEADS])
        kvbias = sb("kvbias", [C + 1, C])
        wq_kb = sb("wq_kb", [C + 1, C])
        lp = sb("lp", [C + 1, C + 1])
        proj = sb("proj", [C + 1, C])
        w_delta = sb("w_delta", [INNER, INNER])
        a_neg = sb("a_neg", [INNER, 2 * STATE])
        diag = sb("diag", [INNER, 2, INNER])
        w_gg = sb("w_gg", [P, 2, 2 * INNER])
        nbias_g = sb("nbias_g", [P, 2])
        w_sim = sb("w_sim", [C, 2 * PK_HEADS * KEYS])

        pix = sb("pix", [P, N * TOK])
        wide = sb("wide", [P, TILES * N * KVW])
        kv = wide[:].rearrange("p (t n w) -> p t n w", t=TILES, n=N)
        scratch = sb("scratch", [P, SCRATCH])
        rf = sb("rf", [P, TILES, C])
        st6 = sb("st6", [P, TILES, 6])
        mv = sb("mv", [P, TILES, 2])
        var = sb("var", [P, TILES * N + TILES])
        lnv = sb("lnv", [P, TILES * N + TILES])
        rstd = sb("rstd", [P, TILES * N + TILES])
        newt = sb("newt", [P, TILES * N + TILES])
        nrm = sb("nrm", [P, TILES, C])
        turned = sb("turned", [C + 1, TOK])
        qs = sb("qs", [P, TILES, C + HEADS])
        sc = sb("sc", [P, TILES * N * HEADS])
        mx = sb("mx", [P, TILES * HEADS])
        den = sb("den", [P, TILES * HEADS])
        h1 = sb("h1", [P, TILES, C])
        ez = wide[:, 0:2 * TOK]
        ez1 = wide[:, 2 * TOK:4 * TOK]
        uz = sb("uz", [INNER, 2, TOK])
        dabs = sb("dabs", [INNER, TOK])
        dlog = sb("dlog", [INNER, TOK])
        delta = sb("delta", [INNER, TOK])
        du = sb("du", [INNER, TOK])
        decay = [sb(f"decay{k}", [INNER, STATE * TOK]) for k in range(2)]
        inject = wide[:, 0:STATE * TOK]
        yg = sb("yg", [INNER, 2, TOK])
        ysum = sb("ysum", [INNER, 2])
        ge = sb("ge", [INNER, 2])
        gate = sb("gate", [INNER, 2])
        wout_g = sb("wout_g", [INNER, 2, C])
        sim = scratch[:, 0:TILES * 2 * PK_HEADS * KEYS].rearrange("p (t j h k) -> p t j h k", t=TILES, j=2, h=PK_HEADS)
        best = sb("best", [P, 2, UNITS, TOPK])
        best_i = sb("best_i", [P, 2, UNITS, TOPK], U32)
        frac = sb("frac", [P, 2, UNITS, TOPK])
        pair = sb("pair", [P, UNITS, PAIRS])
        pair_row = sb("pair_row", [P, UNITS, PAIRS])
        fin = sb("fin", [P, UNITS, TOPK])
        fin_i = sb("fin_i", [P, UNITS, TOPK], U32)
        fin_p = sb("fin_p", [P, UNITS, TOPK])
        row_f = sb("row_f", [P, UNITS, TOPK])
        wexp = sb("wexp", [P, UNITS, TOPK])
        wden = sb("wden", [P, UNITS])
        rows = [sb(f"rows{k}", [P, UNITS * TOPK], U32) for k in range(2)]
        wts = [sb(f"wts{k}", [P, UNITS, TOPK]) for k in range(2)]
        acc = [sb(f"acc{k}", [P, TILES, C]) for k in range(2)]
        xT = [sb(f"xT{k}", [C, TOK]) for k in range(2)]
        kvT = sb("kvT", [P, 2, TOK])
        qT = sb("qT", [C, TOK])
        vo = sb("vo", [P, TILES, C])
        negmax = sb("negmax", [P, TILES])
        rowsum = sb("rowsum", [P, TILES])
        rrow = sb("rrow", [P, TILES])
        prob = sb("prob", [P, 3 * P])
        probT = sb("probT", [P, 3 * P])

        loads = sem("loads")
        w_mm = sem("w_mm")
        w_dve = sem("w_dve")
        w_act = sem("w_act")
        x_loaded = sem("x_loaded")
        x_squared = sem("x_squared")
        rf_ready = sem("rf_ready")
        kv_ready = sem("kv_ready")
        kv_copied = sem("kv_copied")
        var_ready = sem("var_ready")
        rsqrt_ready = sem("rsqrt_ready")
        nrm_ready = sem("nrm_ready")
        turn_ready = sem("turn_ready")
        turn_copied = sem("turn_copied")
        q_ready = sem("q_ready")
        proj_ready = sem("proj_ready")
        scores_ready = sem("scores_ready")
        probs_ready = sem("probs_ready")
        xz_ready = sem("xz_ready")
        xz_exp = sem("xz_exp")
        uz_ready = sem("uz_ready")
        dt_ready = sem("dt_ready")
        dt_log = sem("dt_log")
        delta_ready = sem("delta_ready")
        bc_ready = sem("bc_ready")
        bc_used = sem("bc_used")
        decay_ready = sem("decay_ready")
        y_ready = sem("y_ready")
        ysum_ready = sem("ysum_ready")
        gate_mm = sem("gate_mm")
        gate_exp = sem("gate_exp")
        wout_ready = sem("wout_ready")
        block_ready = sem("block_ready")
        sim_ready = sem("sim_ready")
        sim_copied = sem("sim_copied")
        pick_ready = sem("pick_ready")
        pick_exp = sem("pick_exp")
        rows_ready = sem("rows_ready")
        wts_ready = sem("wts_ready")
        gathered = [sem(f"gathered{k}") for k in range(SLOTS)]
        weighted = sem("weighted")
        summed = sem("summed")
        kvT_copied = sem("kvT_copied")
        qT_ready = sem("qT_ready")
        qT_copied = sem("qT_copied")
        vo_ready = sem("vo_ready")
        vo_copied = sem("vo_copied")
        s_ready = sem("s_ready")
        max_ready = sem("max_ready")
        p_ready = sem("p_ready")
        pT_ready = sem("pT_ready")
        pT_copied = sem("pT_copied")
        o_ready = sem("o_ready")
        acc_ready = sem("acc_ready")
        stored = sem("stored")
        held = sem("held")
        dve_step = sem("dve_step")
        act_step = sem("act_step")


        NLOAD = 27

        block = ctx.enter_context(nc.Block())

        @block.sync
        def _(sp):
            for dst, src in (
                    (ident[:], ident_d), (causal[:], causal_d), (pos[:], pos_d), (headoff[:], headoff_d),
                    (wkv_raw[:], wkvT), (lnkv_s[:], lnkv), (wq_raw[:], wqT), (lnq_s[:], lnq),
                    (proj_raw[:], projE), (w_in[:], w_inT), (wx_rows[:], w_x[0:RANK, :]),
                    (wx_cols[:], w_xT), (wdt[:], w_dtT), (bdt[:], b_dt), (alog[:], a_log),
                    (dskip[:], d_skip), (wglob, w_global.rearrange("(k p) m -> p k m", p=P)),
                    (wgate, w_gateT.rearrange("(k p) m -> p k m", p=P)),
                    (bglob[:], b_global), (bgate[:], b_gate),
                    (wout[:], w_outT.rearrange("(k p) m -> p k m", p=P)),
                    (wqpk, wq_pkT), (pkk, pk_keysT), (wq_ffn[:], w_q),
                    (wo_ffn[C:P, :, :], w_o.rearrange("(h d) c -> d h c", d=C)),
                    (pix[0:C, :], x[0]), (pix[C:P, :], x[0])):
                sp.dma_start(dst, src).then_inc(loads, 16)

            def load_image(a):
                sp.wait_ge(kv_ready, a * NKV)
                sp.dma_start(pix[0:C, :], x[a]).then_inc(x_loaded, 16)
                sp.dma_start(pix[C:P, :], x[a]).then_inc(x_loaded, 16)

            def store_image(b, k):
                sp.wait_ge(acc_ready, b * PK_HEADS + PK_HEADS)
                sp.dma_start(out[b].rearrange("(t p) c -> p t c", p=P), acc[k][:]).then_inc(stored, 16)

            load_image(1)
            store_image(0, 0)
            with sp.Fori(0, IMAGES // 2 - 1) as i:
                load_image(i * 2 + 2)
                store_image(i * 2 + 1, 1)
                load_image(i * 2 + 3)
                store_image(i * 2 + 2, 0)
            store_image(IMAGES - 1, 1)
            sp.wait_ge(stored, 16 * IMAGES)

        @block.gpsimd
        def _(pool):
            def gather_image(b, k):
                for u in range(UNITS):
                    if u == 0:
                        pool.wait_ge(rows_ready, b + 1)
                    if u >= SLOTS:
                        pool.wait_ge(summed, b * UNITS + (u - SLOTS + 1))
                    elif not (isinstance(b, int) and b == 0):
                        pool.wait_ge(summed, b * UNITS + (u - SLOTS + 1))
                    pool.sem_inc(held, 1)
                    for j in range(TOPK):
                        pool.indirect_dma_start(
                            out=gath[:, u % SLOTS, j, :], out_offset=None, in_=table,
                            in_offset=bass.IndirectOffsetOnAxis(
                                ap=rows[k][:, u * TOPK + j:u * TOPK + j + 1], axis=0),
                        ).then_inc(gathered[u % SLOTS], 16)

            gather_image(0, 0)
            with pool.Fori(0, IMAGES // 2 - 1) as i:
                gather_image(i * 2 + 1, 1)
                gather_image(i * 2 + 2, 0)
            gather_image(IMAGES - 1, 1)

        @block.tensor
        def _(pe):
            mm = nc.tensor.matmul

            def prepare():
                pe.wait_ge(w_dve, 1)
                mm(small_ps[0:C, 0:2 * C], ones64[:], wkv[0:C, 0:2 * C], start=True, stop=True)
                mm(small_ps[0:C + 1, 128:192], lnkv_s[:, 1:2].to_broadcast([C, C + 1]), wkv_raw[:, 0:C],
                   start=True, stop=True)
                mm(small_ps[0:C, 192:193], wkv_raw[:, C:2 * C], lnkv_s[:, 1:2], start=True, stop=True)
                mm(small_ps[0:C + 1, 256:320], lq[:], wq_raw[:], start=True, stop=True)
                mm(small_ps[:, 320:448], wx_rows[:], wdt[:], start=True, stop=True).then_inc(w_mm, 1)
                for k in range(2):
                    for j in range(2):
                        mm(scan_ps[:, k * 256:(k + 1) * 256], wglob[:, j, k * P:(k + 1) * P], wgate[:, j, :],
                           start=(j == 0), stop=(j == 1))
                for m in range(2):
                    for j in range(2):
                        mm(turn_ps[:, m:m + 1], wgate[:, j, m * P:(m + 1) * P], bglob[:, j:j + 1],
                           start=(j == 0), stop=(j == 1))
                for g in range(2 * PK_HEADS):
                    last = mm(big_ps[g // 8][0:C, g % 8 * KEYS:(g % 8 + 1) * KEYS],
                              wqpk[:, g * C:(g + 1) * C], pkk[:, g * KEYS:(g + 1) * KEYS],
                              start=True, stop=True)
                last.then_inc(w_mm, 1)
                pe.wait_ge(w_dve, 2)
                pe.wait_ge(w_act, 2)
                mm(small_ps[0:C + 1, 448:512], lp[:], proj_raw[:], start=True, stop=True).then_inc(w_mm, 1)
                pe.wait_ge(w_dve, 3)

            def turn(a, n):
                pe.wait_ge(nrm_ready, a * 4 + (n + 1))
                pe.sem_inc(held, 1)
                for t in range(TILES):
                    last = pe.transpose(turn_ps[0:C, t * P:(t + 1) * P], nrm[:, t, :], ident[:])
                last.then_inc(turn_ready, 1)

            def front(a, k, s):
                first = isinstance(a, int) and a == 0
                if s == 0:
                    if first:
                        pe.wait_ge(x_squared, 1)
                    else:
                        pe.wait_ge(x_squared, a * 1 + 1)
                    pe.sem_inc(held, 1)
                    for t in range(TILES):
                        for n in range(N):
                            last = mm(small_ps[:, t * C:(t + 1) * C],
                                      pix[0:C, n * TOK + t * P:n * TOK + (t + 1) * P], mean16[:],
                                      start=(n == 0), stop=(n == N - 1))
                    last.then_inc(rf_ready, 1)
                if s in (0, 1):
                    t = s
                    for j, (n0, w) in enumerate(KV_CHUNKS):
                        c = t * len(KV_CHUNKS) + j
                        if c >= 2:
                            pe.wait_ge(kv_copied, a * NKV + (c - 1))
                        elif not first:
                            pe.wait_ge(sim_copied, a * 4)
                        for n in range(n0, n0 + w):
                            last = mm(big_ps[c % 2][:, (n - n0) * KVW:(n - n0 + 1) * KVW],
                                      pix[:, n * TOK + t * P:n * TOK + (t + 1) * P], wkv[:],
                                      start=True, stop=True)
                        last.then_inc(kv_ready, 1)
                if s == 2:
                    turn(a, 0)
                    pe.wait_ge(turn_copied, a * 4 + 1)
                    for t in range(TILES):
                        last = mm(small_ps[:, 128 + t * 72:200 + t * 72], turned[:, t * P:(t + 1) * P], wq[:],
                                  start=True, stop=True)
                    last.then_inc(q_ready, 1)
                if s == 3:
                    turn(a, 1)
                    pe.wait_ge(turn_copied, a * 4 + 2)
                    for t in range(TILES):
                        last = mm(small_ps[:, 272 + t * C:272 + (t + 1) * C], turned[:, t * P:(t + 1) * P],
                                  proj[:], start=True, stop=True)
                    last.then_inc(proj_ready, 1)
                if s == 4:
                    turn(a, 2)
                    pe.wait_ge(turn_copied, a * 4 + 3)
                    for j in range(2):
                        last = mm(scan_ps[:, j * TOK:(j + 1) * TOK], w_in[:, j * INNER:(j + 1) * INNER],
                                  turned[0:C, :], start=True, stop=True)
                    last.then_inc(xz_ready, 1)
                    pe.wait_ge(uz_ready, a * 1 + 1)
                    mm(scan_ps[:, 0:TOK], w_delta[:], uz[:, 0, :], start=True, stop=True).then_inc(dt_ready, 1)
                if s in (5, 7):
                    for c in range(NBC):
                        m = c + (NBC if s == 7 else 0)
                        if m >= 2:
                            pe.wait_ge(bc_used, a * 2 * NBC + (m - 1))
                        for j in range(2):
                            n = 2 * c + j
                            col = RANK + n + (STATE if s == 7 else 0)
                            last = mm(big_ps[m % 2][:, j * TOK:(j + 1) * TOK],
                                      wx_cols[:, col:col + 1].to_broadcast([INNER, INNER]), uz[:, 0, :],
                                      start=True, stop=True)
                        last.then_inc(bc_ready, 1)
                if s == 8:
                    pe.wait_ge(bc_used, a * 2 * NBC + 2 * NBC)
                    for r in range(2):
                        for n in range(STATE):
                            mm(scan_ps[:, r * TOK:(r + 1) * TOK], ident[:], decay[r][:, n * TOK:(n + 1) * TOK],
                               start=(n == 0), stop=False)
                        last = mm(scan_ps[:, r * TOK:(r + 1) * TOK], diag[:, r, :], uz[:, 0, :],
                                  start=False, stop=True)
                    last.then_inc(y_ready, 1)
                if s == 9:
                    pe.wait_ge(ysum_ready, a * 1 + 1)
                    for m in range(2):
                        for j in range(2):
                            last = mm(turn_ps[:, 384 + m:385 + m], w_gg[:, j, m * P:(m + 1) * P],
                                      ysum[:, j:j + 1], start=(j == 0), stop=(j == 1))
                    last.then_inc(gate_mm, 1)
                    pe.wait_ge(wout_ready, a * 1 + 1)
                    for t in range(TILES):
                        for j in range(2):
                            last = mm(turn_ps[:, 256 + t * C:256 + (t + 1) * C], yg[:, j, t * P:(t + 1) * P],
                                      wout_g[:, j, :], start=(j == 0), stop=(j == 1))
                    last.then_inc(block_ready, 1)
                if s == 10:
                    turn(a, 3)
                    pe.wait_ge(turn_copied, a * 4 + 4)
                    for t in range(TILES):
                        for j in range(2):
                            if t > 0:
                                pe.wait_ge(sim_copied, a * 4 + (j + 1))
                            mm(big_ps[j][:], xT[k][:, t * P:(t + 1) * P], w_sim[:, j * 512:(j + 1) * 512],
                               start=True, stop=True).then_inc(sim_ready, 1)

            def unit(b, k, u):
                pe.wait_ge(weighted, b * UNITS + (u + 1))
                if u >= 1 or not (isinstance(b, int) and b == 0):
                    pe.wait_ge(kvT_copied, b * UNITS + u)
                q = u % 4
                for j in range(TOPK):
                    last = mm(sum_ps[:, q * P:(q + 1) * P], gath[:, u % SLOTS, j, :], ident[:],
                              start=(j == 0), stop=(j == TOPK - 1))
                last.then_inc(summed, 1)

            def head(b, k, h):
                started = h > 0 or not (isinstance(b, int) and b == 0)
                n = b * PK_HEADS + h
                kvh = kvT[:, h % 2, :]
                if started:
                    pe.wait_ge(acc_ready, n)
                pe.sem_inc(held, 1)
                mm(prob_ps[0:C, 0:TOK], wq_ffn[:, h * C:(h + 1) * C], xT[k][:],
                   start=True, stop=True).then_inc(qT_ready, 1)
                pe.wait_ge(kvT_copied, b * UNITS + (2 * h + 2))
                for t in range(TILES):
                    last = mm(score_ps[:, 384 + t * C:384 + (t + 1) * C], kvh[C:P, t * P:(t + 1) * P],
                              wo_ffn[C:P, h, :], start=True, stop=True)
                last.then_inc(vo_ready, 1)
                pe.wait_ge(qT_copied, n + 1)
                pe.wait_ge(vo_copied, n + 1)
                mm(score_ps[:, 0:P], qT[:, 0:P], kvh[0:C, 0:P], start=True, stop=False)
                mm(score_ps[:, 0:P], ident[:], causal[:], start=False, stop=True)
                mm(score_ps[:, P:3 * P], qT[:, P:TOK], kvh[0:C, :], start=True, stop=False)
                mm(score_ps[:, 2 * P:3 * P], ident[:], causal[:], start=False, stop=True).then_inc(s_ready, 1)
                pe.wait_ge(p_ready, n + 1)
                pe.sem_inc(held, 1)
                for j in range(3):
                    last = pe.transpose(prob_ps[:, j * P:(j + 1) * P], prob[:, j * P:(j + 1) * P], ident[:])
                last.then_inc(pT_ready, 1)
                pe.wait_ge(pT_copied, n + 1)
                mm(prob_ps[:, 384:448], probT[:, 0:P], vo[:, 0, :], start=True, stop=True)
                mm(prob_ps[:, 448:512], probT[:, P:2 * P], vo[:, 0, :], start=True, stop=False)
                mm(prob_ps[:, 448:512], probT[:, 2 * P:3 * P], vo[:, 1, :],
                   start=False, stop=True).then_inc(o_ready, 1)

            def image(b, k, more):
                for u in range(UNITS):
                    if more:
                        front(b + 1, 1 - k, u)
                    unit(b, k, u)
                    if u % 2:
                        head(b, k, u // 2)

            prepare()
            for s in range(UNITS):
                front(0, 0, s)
            image(0, 0, True)
            with pe.Fori(0, IMAGES // 2 - 1) as i:
                image(i * 2 + 1, 1, True)
                image(i * 2 + 2, 0, True)
            image(IMAGES - 1, 1, False)

        @block.scalar
        def _(act):
            af = nc.scalar.activation
            count = [0]

            def step(ins):
                count[0] += 1
                return ins.then_inc(act_step, 1)

            def settle():
                act.wait_ge(act_step, count[0])

            def prepare():
                act.wait_ge(loads, 16 * NLOAD)
                af(a_neg[:], alog[:], ACT.Exp).then_inc(w_act, 1)
                act.wait_ge(w_dve, 2)
                af(w_delta[:], small_ps[:, 320:448], ACT.Copy).then_inc(w_act, 1)
                act.wait_ge(w_mm, 2)
                af(w_gg[:].rearrange("p k m -> p (k m)"), scan_ps[:], ACT.Copy).then_inc(w_act, 1)
                for j in range(2):
                    af(w_sim[:, j * 512:(j + 1) * 512], big_ps[j][0:C, :], ACT.Copy).then_inc(w_act, 1)

            def turn_copy(a, n, dst):
                act.wait_ge(turn_ready, a * 4 + (n + 1))
                af(dst, turn_ps[0:C, 0:TOK], ACT.Copy).then_inc(turn_copied, 1)

            def rsqrt(a, n, w):
                act.wait_ge(var_ready, a * 3 + (n + 1))
                step(af(lnv[:, 0:w], var[:, 0:w], ACT.Ln))
                settle()
                af(rstd[:, 0:w], lnv[:, 0:w], ACT.Exp, scale=-0.5).then_inc(rsqrt_ready, 1)

            def front(a, k, s):
                first = isinstance(a, int) and a == 0
                if s == 0:
                    if not first:
                        act.wait_ge(x_loaded, a * 32)
                    af(pix[C:P, :], pix[C:P, :], ACT.Square).then_inc(x_squared, 1)
                if s in (0, 1):
                    for j, (n0, w) in enumerate(KV_CHUNKS):
                        c = s * len(KV_CHUNKS) + j
                        act.wait_ge(kv_ready, a * NKV + (c + 1))
                        af(kv[:, s, n0:n0 + w, :].rearrange("p n w -> p (n w)"), big_ps[c % 2][:, 0:w * KVW],
                           ACT.Copy).then_inc(kv_copied, 1)
                if s == 1:
                    rsqrt(a, 0, TILES * N + TILES)
                if s == 2:
                    turn_copy(a, 0, turned[0:C, :])
                    act.wait_ge(scores_ready, a * 1 + 1)
                    af(sc[:], sc[:], ACT.Exp, scale=C ** -0.5).then_inc(probs_ready, 1)
                if s == 3:
                    turn_copy(a, 1, turned[0:C, :])
                    rsqrt(a, 1, TILES)
                if s == 4:
                    turn_copy(a, 2, turned[0:C, :])
                    act.wait_ge(xz_ready, a * 1 + 1)
                    af(ez, scan_ps[:], ACT.Exp, scale=-1.0).then_inc(xz_exp, 1)
                    act.wait_ge(dt_ready, a * 1 + 1)
                    step(af(dabs[:], scan_ps[:, 0:TOK], ACT.Abs, bias=bdt[:, 0:1]))
                    settle()
                    step(af(dlog[:], dabs[:], ACT.Exp, scale=-1.0))
                    settle()
                    af(dlog[:], dlog[:], ACT.Ln, bias=1.0).then_inc(dt_log, 1)
                if s == 5:
                    act.wait_ge(delta_ready, a * 1 + 1)
                    for r in range(2):
                        for n in range(STATE):
                            last = af(decay[r][:, n * TOK + 1 - r:(n + 1) * TOK - r], delta[:, 1 - r:TOK - r],
                                      ACT.Exp, scale=a_neg[:, r * STATE + n:r * STATE + n + 1])
                        last.then_inc(decay_ready, 1)
                if s == 9:
                    act.wait_ge(gate_mm, a * 1 + 1)
                    for m in range(2):
                        last = af(ge[:, m:m + 1], turn_ps[:, 384 + m:385 + m], ACT.Exp, scale=-1.0 / TOK,
                                  bias=nbias_g[:, m:m + 1])
                    last.then_inc(gate_exp, 1)
                    rsqrt(a, 2, TILES)
                if s == 10:
                    turn_copy(a, 3, xT[k][:])
                    for t in range(TILES):
                        for j in range(2):
                            act.wait_ge(sim_ready, a * 4 + (2 * t + j + 1))
                            af(sim[:, t, j, :, :].rearrange("p h k -> p (h k)"), big_ps[j][:],
                               ACT.Copy).then_inc(sim_copied, 1)
                if s == 14:
                    act.wait_ge(pick_ready, a * 1 + 1)
                    af(wexp[:], wexp[:], ACT.Exp).then_inc(pick_exp, 1)

            def unit(b, k, u):
                act.wait_ge(gathered[u % SLOTS], b * (UNITS // SLOTS * TOPK * 16) + (u // SLOTS + 1) * TOPK * 16)
                if u == 0:
                    act.wait_ge(wts_ready, b * 1 + 1)
                for j in range(TOPK):
                    last = af(gath[:, u % SLOTS, j, :], gath[:, u % SLOTS, j, :], ACT.Copy,
                              scale=wts[k][:, u, j:j + 1])
                last.then_inc(weighted, 1)
                act.wait_ge(summed, b * UNITS + (u + 1))
                if u < 4 and not (isinstance(b, int) and b == 0):
                    act.wait_ge(s_ready, b * PK_HEADS + (u // 2 - 1))
                elif u >= 4:
                    act.wait_ge(s_ready, b * PK_HEADS + (u // 2 - 1))
                af(kvT[:, u // 2 % 2, u % 2 * P:(u % 2 + 1) * P], sum_ps[:, u % 4 * P:(u % 4 + 1) * P],
                   ACT.Copy).then_inc(kvT_copied, 1)

            def head(b, k, h):
                started = h > 0 or not (isinstance(b, int) and b == 0)
                n = b * PK_HEADS + h
                act.wait_ge(qT_ready, n + 1)
                af(qT[:], prob_ps[0:C, 0:TOK], ACT.Copy, scale=C ** -0.5).then_inc(qT_copied, 1)
                act.wait_ge(max_ready, n + 1)
                if started:
                    act.wait_ge(pT_ready, n)
                af(prob[:, 0:P], score_ps[:, 0:P], ACT.Exp, bias=negmax[:, 0:1], accum_out=rowsum[:, 0:1])
                af(prob[:, P:3 * P], score_ps[:, P:3 * P], ACT.Exp, bias=negmax[:, 1:2],
                   accum_out=rowsum[:, 1:2]).then_inc(p_ready, 1)
                act.wait_ge(pT_ready, n + 1)
                if started:
                    act.wait_ge(o_ready, n)
                af(probT[:], prob_ps[:, 0:3 * P], ACT.Copy).then_inc(pT_copied, 1)

            def new_image():
                settle()
                act.sem_clear(act_step)
                count[0] = 0

            def image(b, k, more):
                if more:
                    new_image()
                for u in range(UNITS):
                    if more:
                        front(b + 1, 1 - k, u)
                    unit(b, k, u)
                    if u % 2:
                        head(b, k, u // 2)

            act.preload_act_table_set("natural_log_exp_and_others")
            prepare()
            for s in range(UNITS):
                front(0, 0, s)
            image(0, 0, True)
            with act.Fori(0, IMAGES // 2 - 1) as i:
                image(i * 2 + 1, 1, True)
                image(i * 2 + 2, 0, True)
            image(IMAGES - 1, 1, False)

        @block.vector
        def _(dve):
            v = nc.vector
            count = [0]

            told = [None]

            def step(ins, sem=None, value=0):
                if sem is None:
                    count[0] += 1
                    told[0] = None
                    return ins.then_inc(dve_step, 1)
                told[0] = (sem, value)
                return ins.then_inc(sem, 1)

            def settle():
                if told[0]:
                    dve.wait_ge(*told[0])
                    told[0] = None
                    alone()
                else:
                    dve.wait_ge(dve_step, count[0])

            def alone():
                dve.sem_inc(held, 1)

            def prepare():
                dve.wait_ge(loads, 16 * NLOAD)
                step(v.memset(wkv[:], 0.0))
                step(v.memset(turned[C:C + 1, :], 1.0))
                step(v.memset(ones64[:], 1.0 / C))
                step(v.tensor_scalar(mean16[:], ident[0:C, 0:C], 1.0 / N, None, ALU.mult))
                step(v.tensor_scalar(lq[:, 0:C], ident[0:C, 0:C], lnq_s[:, 0:1], None, ALU.mult))
                step(v.tensor_copy(lq[:, C:C + 1], lnq_s[:, 1:2]))
                step(v.tensor_copy(lp[:], ident[0:C + 1, 0:C + 1]))
                for r in range(2):
                    step(v.tensor_scalar(diag[:, r, :], ident[:], dskip[:, r:r + 1], None, ALU.mult))
                settle()
                step(v.memset(wkv[C:P, 2 * C:2 * C + 1], 1.0 / C))
                step(v.memset(wkv[0:C, 2 * C + 1:2 * C + 2], 1.0 / C))
                step(v.tensor_scalar(wkv[0:C, 0:2 * C], wkv_raw[:], lnkv_s[:, 0:1], None, ALU.mult))
                settle()
                step(v.tensor_copy(ysum[:], dskip[:]), w_dve, 1)
                dve.wait_ge(w_act, 1)
                step(v.tensor_scalar(a_neg[:], a_neg[:], -1.0, None, ALU.mult))
                dve.wait_ge(w_mm, 1)
                step(v.tensor_tensor(wkv[0:C, 0:2 * C], wkv[0:C, 0:2 * C], small_ps[0:C, 0:2 * C], ALU.subtract))
                step(v.tensor_copy(kvbias[:], small_ps[0:C + 1, 128:192]))
                step(v.tensor_copy(wq[:, 0:C], small_ps[0:C + 1, 256:320]))
                step(v.tensor_copy(lp[0:C, C:C + 1], small_ps[0:C, 192:193]))
                settle()
                step(v.tensor_tensor(wq_kb[:], wq[:, 0:C], kvbias[:], ALU.mult), w_dve, 2)
                settle()
                step(v.tensor_reduce(wq[:, C:C + HEADS], wq_kb[:].rearrange("p (h d) -> p h d", d=D), AX, ALU.add))
                dve.wait_ge(w_mm, 2)
                step(v.tensor_tensor(nbias_g[:], turn_ps[:, 0:2], bgate[:], ALU.add))
                settle()
                step(v.tensor_scalar(nbias_g[:], nbias_g[:], -1.0, None, ALU.mult))
                dve.wait_ge(w_mm, 3)
                dve.wait_ge(w_act, 5)
                step(v.tensor_copy(proj[:], small_ps[0:C + 1, 448:512]))
                settle()
                step(v.tensor_copy(mx[:, 0:2], dskip[:]), w_dve, 3)
                settle()

            def newton(a, n, w):
                dve.wait_ge(rsqrt_ready, a * 3 + (n + 1))
                step(v.scalar_tensor_tensor(newt[:, 0:w], rstd[:, 0:w], -0.5, rstd[:, 0:w], ALU.mult, ALU.mult))
                settle()
                step(v.tensor_tensor(newt[:, 0:w], newt[:, 0:w], var[:, 0:w], ALU.mult))
                settle()
                step(v.scalar_tensor_tensor(rstd[:, 0:w], newt[:, 0:w], 1.5, rstd[:, 0:w], ALU.add, ALU.mult))
                settle()

            def moments(src, at, *signal):
                for t in range(TILES):
                    step(v.bn_stats(st6[:, t, :], src[t]))
                settle()
                for t in range(TILES):
                    step(v.bn_aggr(mv[:, t, :], st6[:, t, :]))
                settle()
                ins = v.tensor_scalar(var[:, at:at + TILES], mv[:, :, 1], EPS, None, ALU.add)
                step(ins, *signal)

            def normalize(src, at, value):
                for t in range(TILES):
                    last = v.tensor_scalar(nrm[:, t, :], src[t], mv[:, t, 0:1], rstd[:, at + t:at + t + 1],
                                           ALU.subtract, ALU.mult)
                step(last, nrm_ready, value)

            def front(a, k, s):
                first = isinstance(a, int) and a == 0
                nt = TILES * N
                if s == 1:
                    dve.wait_ge(rf_ready, a * 1 + 1)
                    step(v.tensor_copy(rf[:].rearrange("p t c -> p (t c)"), small_ps[:, 0:TILES * C]))
                    settle()
                    moments([rf[:, t, :] for t in range(TILES)], nt)
                    dve.wait_ge(kv_copied, a * NKV + NKV)
                    kvf = wide[:].rearrange("p (m w) -> p m w", w=KVW)
                    step(v.tensor_tensor(newt[:, 0:nt], kvf[:, :, 2 * C + 1], kvf[:, :, 2 * C + 1], ALU.mult))
                    settle()
                    step(v.scalar_tensor_tensor(var[:, 0:nt], kvf[:, :, 2 * C], EPS, newt[:, 0:nt],
                                                ALU.add, ALU.subtract), var_ready, a * 3 + 1)
                    newton(a, 0, nt + TILES)
                    normalize([rf[:, t, :] for t in range(TILES)], nt, a * 4 + 1)
                if s == 2:
                    dve.wait_ge(q_ready, a * 1 + 1)
                    step(v.tensor_copy(qs[:].rearrange("p t c -> p (t c)"), small_ps[:, 128:272]))
                    settle()
                    prod = scratch[:, 0:nt * C].rearrange("p (t n c) -> p t n c", t=TILES, n=N)
                    step(v.tensor_tensor(prod, kv[:, :, :, 0:C],
                                         qs[:, :, 0:C].unsqueeze(2).to_broadcast([P, TILES, N, C]), ALU.mult))
                    settle()
                    step(v.tensor_reduce(sc[:], scratch[:, 0:nt * C].rearrange("p (m d) -> p m d", d=D), AX, ALU.add))
                    settle()
                    sc3 = sc[:].rearrange("p (m h) -> p m h", h=HEADS)
                    sc4 = sc[:].rearrange("p (t n h) -> p t n h", t=TILES, h=HEADS)
                    rs3 = rstd[:, 0:nt].unsqueeze(2).to_broadcast([P, nt, HEADS])
                    step(v.tensor_tensor(sc3, sc3, rs3, ALU.mult))
                    settle()
                    step(v.tensor_tensor(sc4, sc4, qs[:, :, C:].unsqueeze(2).to_broadcast([P, TILES, N, HEADS]),
                                         ALU.add))
                    settle()
                    by_n = sc[:].rearrange("p (t n h) -> p t h n", t=TILES, h=HEADS)
                    mx3 = mx[:].rearrange("p (t h) -> p t h", t=TILES)
                    den3 = den[:].rearrange("p (t h) -> p t h", t=TILES)
                    step(v.tensor_reduce(mx3, by_n, AX, ALU.max))
                    settle()
                    step(v.tensor_tensor(sc4, sc4, mx3.unsqueeze(2).to_broadcast([P, TILES, N, HEADS]),
                                         ALU.subtract), scores_ready, a + 1)
                    dve.wait_ge(probs_ready, a * 1 + 1)
                    step(v.tensor_reduce(den3, by_n, AX, ALU.add))
                    settle()
                    step(v.reciprocal(den[:], den[:]))
                    step(v.tensor_tensor(sc3, sc3, rs3, ALU.mult))
                    settle()
                    step(v.tensor_tensor(scratch[:, 0:nt * C].rearrange("p (m h d) -> p m h d", h=HEADS, d=D),
                                         wide[:].rearrange("p (m w) -> p m w", w=KVW)[:, :, C:2 * C]
                                         .rearrange("p m (h d) -> p m h d", d=D),
                                         sc3.unsqueeze(3).to_broadcast([P, nt, HEADS, D]), ALU.mult))
                    settle()
                    step(v.tensor_reduce(nrm[:], scratch[:, 0:nt * C].rearrange("p (t n c) -> p t c n", t=TILES, n=N),
                                         AX, ALU.add))
                    settle()
                    nh = nrm[:].rearrange("p t (h d) -> p (t h) d", d=D)
                    step(v.tensor_tensor(nh, nh, den[:].unsqueeze(2).to_broadcast([P, TILES * HEADS, D]),
                                         ALU.mult), nrm_ready, a * 4 + 2)
                if s == 3:
                    dve.wait_ge(proj_ready, a * 1 + 1)
                    step(v.tensor_tensor(h1[:].rearrange("p t c -> p (t c)"), small_ps[:, 272:400],
                                         rf[:].rearrange("p t c -> p (t c)"), ALU.add))
                    settle()
                    moments([h1[:, t, :] for t in range(TILES)], 0, var_ready, a * 3 + 2)
                    newton(a, 1, TILES)
                    normalize([h1[:, t, :] for t in range(TILES)], 0, a * 4 + 3)
                if s == 4:
                    dve.wait_ge(xz_exp, a * 1 + 1)
                    step(v.tensor_scalar(ez1, ez, 1.0, None, ALU.add))
                    settle()
                    step(v.reciprocal(ez1, ez1))
                    settle()
                    step(v.tensor_tensor(uz[:].rearrange("p j l -> p (j l)"), scan_ps[:], ez1,
                                         ALU.mult), uz_ready, a + 1)
                    for r in range(2):
                        first_col = decay[r][:].rearrange("p (n l) -> p n l", l=TOK)
                        step(v.memset(first_col[:, :, 0 if r == 0 else TOK - 1], 0.0))
                    dve.wait_ge(dt_ready, a * 1 + 1)
                    dve.wait_ge(dt_log, a * 1 + 1)
                    step(v.tensor_scalar(delta[:], scan_ps[:, 0:TOK], bdt[:, 0:1], 0.0, ALU.add, ALU.max))
                    settle()
                    step(v.tensor_tensor(delta[:], delta[:], dlog[:], ALU.add), delta_ready, a + 1)
                    settle()
                    step(v.tensor_tensor(du[:], delta[:], uz[:, 0, :], ALU.mult))
                    settle()
                if s == 5:
                    for c in range(NBC):
                        dve.wait_ge(bc_ready, a * 2 * NBC + (c + 1))
                        step(v.tensor_tensor(inject[:, c * 512:(c + 1) * 512].rearrange("p (j l) -> p j l", j=2),
                                             big_ps[c % 2][:].rearrange("p (j l) -> p j l", j=2),
                                             du[:].unsqueeze(1).to_broadcast([INNER, 2, TOK]),
                                             ALU.mult), bc_used, a * 2 * NBC + (c + 1))
                if s == 6:
                    settle()
                    dve.wait_ge(decay_ready, a * 2 + 1)
                    step(v.tensor_tensor_scan(decay[0][:], decay[0][:], inject, 0.0, ALU.mult, ALU.add))
                    dve.wait_ge(decay_ready, a * 2 + 2)
                    step(v.tensor_tensor_scan(decay[1][:, ::-1], decay[1][:, ::-1], inject[:, ::-1], 0.0,
                                              ALU.mult, ALU.add))
                if s == 7:
                    settle()
                    for c in range(NBC):
                        m = NBC + c
                        dve.wait_ge(bc_ready, a * 2 * NBC + (m + 1))
                        for r in range(2):
                            hs = decay[r][:, c * 512:(c + 1) * 512]
                            last = v.tensor_tensor(hs, hs, big_ps[m % 2][:], ALU.mult)
                        step(last, bc_used, a * 2 * NBC + (m + 1))
                if s == 9:
                    dve.wait_ge(y_ready, a * 1 + 1)
                    step(v.tensor_tensor(yg[:], scan_ps[:].rearrange("p (r l) -> p r l", r=2),
                                         uz[:, 1, :].unsqueeze(1).to_broadcast([INNER, 2, TOK]), ALU.mult))
                    settle()
                    step(v.tensor_reduce(ysum[:], yg[:], AX, ALU.add), ysum_ready, a + 1)
                    dve.wait_ge(gate_exp, a * 1 + 1)
                    step(v.tensor_scalar(gate[:], ge[:], 1.0, None, ALU.add))
                    settle()
                    step(v.reciprocal(gate[:], gate[:]))
                    settle()
                    for j in range(2):
                        last = v.tensor_scalar(wout_g[:, j, :], wout[:, j, :], gate[:, j:j + 1], None, ALU.mult)
                    step(last, wout_ready, a + 1)
                    dve.wait_ge(block_ready, a * 1 + 1)
                    if isinstance(a, int) and a < 2:
                        pass
                    else:
                        dve.wait_ge(stored, (a - 1) * 16)
                    settle()
                    step(v.tensor_tensor(acc[k][:].rearrange("p t c -> p (t c)"), turn_ps[:, 256:384],
                                         h1[:].rearrange("p t c -> p (t c)"), ALU.add))
                    settle()
                    moments([acc[k][:, t, :] for t in range(TILES)], 0, var_ready, a * 3 + 3)
                    newton(a, 2, TILES)
                    normalize([acc[k][:, t, :] for t in range(TILES)], 0, a * 4 + 4)
                if s in (11, 12):
                    t = s - 11
                    settle()
                    dve.wait_ge(sim_copied, a * 4 + 2 * (t + 1))
                    alone()
                    lists = [(sim[:, t, j, h, :], best[:, j, h * TILES + t, :], best_i[:, j, h * TILES + t, :])
                             for j in range(2) for h in range(PK_HEADS)]
                    top16(lists)
                if s == 13:
                    settle()
                    step(v.tensor_scalar(frac[:, 0], best_i[:, 0], FRAC, None, ALU.mult))
                    step(v.tensor_scalar(frac[:, 1], best_i[:, 1], FRAC * KEYS, None, ALU.mult))
                    for r0, rw, cw, p0 in STAIRS:
                        dst = pair[:, :, p0:p0 + rw * cw].rearrange("p u (r c) -> p u r c", c=cw)
                        step(v.tensor_tensor(dst, best[:, 0, :, r0:r0 + rw].unsqueeze(3).to_broadcast([P, UNITS, rw, cw]),
                                             best[:, 1, :, 0:cw].unsqueeze(2).to_broadcast([P, UNITS, rw, cw]), ALU.add))
                    settle()
                    for r0, rw, cw, p0 in STAIRS:
                        dst = pair_row[:, :, p0:p0 + rw * cw].rearrange("p u (r c) -> p u r c", c=cw)
                        step(v.tensor_tensor(dst, frac[:, 0, :, r0:r0 + rw].unsqueeze(3).to_broadcast([P, UNITS, rw, cw]),
                                             frac[:, 1, :, 0:cw].unsqueeze(2).to_broadcast([P, UNITS, rw, cw]), ALU.add))
                    settle()
                    step(v.tensor_tensor(pair_row[:], pair_row[:],
                                         pos[:].unsqueeze(1).to_broadcast([P, UNITS, PAIRS]), ALU.add))
                    top16([(pair[:, u, :], fin[:, u, :], fin_i[:, u, :]) for u in range(UNITS)])
                if s == 14:
                    settle()
                    step(v.tensor_copy(fin_p[:], fin_i[:]))
                    step(v.tensor_tensor(wexp[:], fin[:], fin[:, :, 0:1].to_broadcast([P, UNITS, TOPK]),
                                         ALU.subtract), pick_ready, a + 1)
                    settle()
                    g = SCRATCH // (TOPK * PAIRS)
                    for u in range(0, UNITS, g):
                        d4 = scratch[:, 0:g * TOPK * PAIRS].rearrange("p (u j e) -> p u j e", u=g, j=TOPK)
                        step(v.tensor_tensor(d4, pair_row[:, u:u + g, :].unsqueeze(2).to_broadcast([P, g, TOPK, PAIRS]),
                                             fin_p[:, u:u + g, :].unsqueeze(3).to_broadcast([P, g, TOPK, PAIRS]),
                                             ALU.subtract))
                        settle()
                        step(v.tensor_reduce(row_f[:, u:u + g, :], d4, AX, ALU.min, apply_absolute_value=True))
                        settle()
                    step(v.scalar_tensor_tensor(rows[k][:], row_f[:].rearrange("p u j -> p (u j)"), 1.0 / FRAC,
                                                headoff[:], ALU.mult, ALU.add), rows_ready, a + 1)
                    dve.wait_ge(pick_exp, a * 1 + 1)
                    step(v.tensor_reduce(wden[:], wexp[:], AX, ALU.add))
                    settle()
                    step(v.reciprocal(wden[:], wden[:]))
                    settle()
                    step(v.tensor_tensor(wts[k][:], wexp[:], wden[:].unsqueeze(2).to_broadcast([P, UNITS, TOPK]),
                                         ALU.mult), wts_ready, a + 1)

            def top16(lists):
                for vals, top, idx in lists:
                    step(v.max(top[:, 0:8], vals))
                settle()
                for vals, top, idx in lists:
                    step(v.max_index(idx[:, 0:8], top[:, 0:8], vals))
                settle()
                for vals, top, idx in lists:
                    step(v.match_replace(vals, top[:, 0:8], vals, -3.0e38))
                settle()
                for vals, top, idx in lists:
                    step(v.max(top[:, 8:16], vals))
                settle()
                for vals, top, idx in lists:
                    step(v.max_index(idx[:, 8:16], top[:, 8:16], vals))

            def head(b, k, h):
                started = h > 0 or not (isinstance(b, int) and b == 0)
                n = b * PK_HEADS + h
                dve.wait_ge(vo_ready, n + 1)
                if started:
                    dve.wait_ge(o_ready, n)
                step(v.tensor_copy(vo[:].rearrange("p t c -> p (t c)"), score_ps[:, 384:512]), vo_copied, n + 1)
                dve.wait_ge(s_ready, n + 1)
                step(v.tensor_reduce(negmax[:, 0:1], score_ps[:, 0:P], AX, ALU.max, negate=True))
                step(v.tensor_reduce(negmax[:, 1:2], score_ps[:, P:3 * P], AX, ALU.max,
                                     negate=True), max_ready, n + 1)
                dve.wait_ge(p_ready, n + 1)
                step(v.reciprocal(rrow[:], rowsum[:]))
                dve.wait_ge(o_ready, n + 1)
                settle()
                for t in range(TILES):
                    last = v.scalar_tensor_tensor(acc[k][:, t, :], prob_ps[:, 384 + t * C:384 + (t + 1) * C],
                                                  rrow[:, t:t + 1], acc[k][:, t, :], ALU.mult, ALU.add)
                step(last, acc_ready, n + 1)

            def new_image():
                settle()
                dve.sem_clear(dve_step)
                count[0] = 0

            def image(b, k, more):
                new_image()
                for u in range(UNITS):
                    if more:
                        front(b + 1, 1 - k, u)
                    if u % 2:
                        head(b, k, u // 2)

            prepare()
            for s in range(UNITS):
                front(0, 0, s)
            image(0, 0, True)
            with dve.Fori(0, IMAGES // 2 - 1) as i:
                image(i * 2 + 1, 1, True)
                image(i * 2 + 2, 0, True)
            image(IMAGES - 1, 1, False)


def kernel(**inputs):
    import concourse.bacc as _bacc
    from concourse.bass_utils import run_bass_kernel_spmd as _run

    g = {k: np.asarray(v) for k, v in inputs.items()}
    tok = lambda n: g["L0_tok_" + n]
    att = lambda n: g["L0_attn_" + n]
    ffn = lambda n: g["L0_ffn_" + n]
    ident, causal, pos, head = host_constants()
    c = np.ascontiguousarray
    arrays = {
        "x": c(g["x"].reshape(64, 64, 16, 4, 16, 4).transpose(0, 1, 3, 5, 2, 4)).reshape(64, 64, 4096),
        "wkvT": c(tok("Wkv").T),
        "lnkv": c(np.stack([tok("ln_kv_w"), tok("ln_kv_b")], 1)),
        "wqT": c(tok("Wq").T),
        "lnq": c(np.stack([tok("ln_q_w"), tok("ln_q_b")], 1)),
        "projE": c(np.concatenate([tok("proj_w").T, tok("proj_b")[None]], 0)),
        "w_inT": c(att("W_in").T),
        "w_x": c(att("W_xproj")),
        "w_xT": c(att("W_xproj").T),
        "w_dtT": c(att("W_dt").T),
        "b_dt": c(att("b_dt")[:, None]),
        "a_log": c(np.concatenate([att("A_log_f"), att("A_log_b")], 1)),
        "d_skip": c(np.stack([att("D_f"), att("D_b")], 1)),
        "w_global": c(att("W_global")),
        "w_gateT": c(att("W_gate").T),
        "b_global": c(att("b_global").reshape(2, 128).T),
        "b_gate": c(att("b_gate").reshape(2, 128).T),
        "w_outT": c(att("W_out").T),
        "wq_pkT": c(ffn("Wq_pk").reshape(64, 16, 32).transpose(2, 1, 0)).reshape(32, 1024),
        "pk_keysT": c(ffn("pk_keys").transpose(3, 0, 2, 1)).reshape(32, 1024),
        "w_q": c(ffn("Wq")),
        "w_o": c(ffn("Wo")),
        "table": c(np.concatenate([ffn("keys_table"), ffn("values_table")], 1)),
        "ident": ident, "causal": causal, "pos": pos, "headoff": head,
    }
    nc = _bacc.Bacc("TRN2", target_bir_lowering=False, num_devices=1)
    named, args = {}, []
    for name, a in arrays.items():
        named[f"in_{name}_dram"] = a
        args.append(nc.dram_tensor(f"in_{name}_dram", a.shape, mybir.dt.from_np(a.dtype), kind="ExternalInput").ap())
    args.append(nc.dram_tensor("out_dram", (IMAGES, TOK, C), F32, kind="ExternalOutput").ap())
    build(nc, *args)
    r = _run(nc, [named], core_ids=[0])
    return r.results[0]["out_dram"]
```

```python
from contextlib import ExitStack

import numpy as np
import concourse.bass as bass
from concourse import mybir

ALU = mybir.AluOpType
ACT = mybir.ActivationFunctionType
AX = mybir.AxisListType.X
F32 = mybir.dt.float32
U32 = mybir.dt.uint32

P = 128
IMAGES = 64
C = 64
SIDE = 16
TOK = SIDE * SIDE
TILES = TOK // P
N = 16
HEADS = 8
D = C // HEADS
INNER = 128
STATE = 16
RANK = 16
PK_HEADS = 8
KEYS = 64
TOPK = 16
EPS = 1e-5
KVW = 2 * C + 2
UNITS = PK_HEADS * TILES
SLOTS = 8
PIECES = 18
ALONE = (6, 11, 12, 13, 14, 15, 16, 17)
ON_ACT = tuple(range(16))
PLAN = [[(1, 2)], [(1, 3), (1, 4)], [(1, 5)], [(1, 6)], [(1, 7)], [(1, 9)], [(1, 10)], [(1, 11)],
        [(1, 12), (2, 0)], [(1, 13)], [(1, 14), (2, 1)], [(1, 15)], [(1, 16)], [(1, 17)], [], []]


def steps(u, left):
    h = u // 2
    pieces = [("front", x) for x in PLAN[u] if x[0] <= left]
    early = not pieces or pieces[0][1][1] in ALONE
    late = u % 2 == 0 and u
    todo = [("weigh", u)]
    todo += [("max", h - 1)] if late else []
    todo += [("sum", u)] if early else []
    todo += [("turn", h - 1)] if late else []
    todo += pieces
    todo += [] if early else [("sum", u)]
    todo += [("add", h - 1)] if late else []
    if u % 2:
        todo += [("scores", h)]
    if u == UNITS - 1:
        todo += [("max", h), ("turn", h), ("add", h)]
    return todo
GROUP = 4

STAIRS = []
_pos = 0
_r = 0
while _r < TOPK:
    _c = TOPK // (_r + 1)
    _rows = 1
    while _r + _rows < TOPK and TOPK // (_r + _rows + 1) == _c:
        _rows += 1
    STAIRS.append((_r, _rows, _c, _pos))
    _pos += _rows * _c
    _r += _rows
PAIRS = _pos
SCRATCH = GROUP * TOPK * PAIRS
FRAC = 1.0 / 16384.0

KV_CHUNKS = [(n, min(3, N - n)) for n in range(0, N, 3)]
NKV = TILES * len(KV_CHUNKS)
NBC = STATE // 2


def host_constants():
    ident = np.eye(P, dtype=np.float32)
    i = np.arange(P)
    causal = np.where(i[None, :] <= i[:, None], 0.0, -1e30).astype(np.float32)
    pos = np.tile(np.arange(PAIRS, dtype=np.float32), (P, 1))
    head = np.repeat(np.arange(UNITS) // TILES * KEYS * KEYS, TOPK).astype(np.float32)
    return ident, causal, np.ascontiguousarray(pos), np.tile(head, (P, 1))


def build(nc, x, wkvT, lnkv, wqT, lnq, projE, w_inT, w_x, w_xT, w_dtT, b_dt, a_log, d_skip,
          w_global, w_gateT, b_global, b_gate, w_outT, wq_pkT, pk_keysT, w_q, w_o, table,
          ident_d, causal_d, pos_d, headoff_d, out):
    with ExitStack() as ctx:
        def sb(name, shape, dt=F32):
            return ctx.enter_context(nc.sbuf_tensor(name, shape, dt))

        def sem(name):
            return ctx.enter_context(nc.semaphore(name))

        bank = [ctx.enter_context(nc.psum_tensor(f"bank{i}", [P, 512], F32)) for i in range(8)]
        big_ps = bank[0:2]
        small_ps = bank[2]
        turn_ps = bank[3]
        scan_ps = bank[4]
        sum_ps = bank[5]
        score_ps = bank[6]
        prob_ps = bank[7]

        gath = sb("gath", [P, SLOTS, TOPK, 2 * C])
        spare = gath[:].rearrange("p s j c -> p (s j c)")
        wglob = spare[:, 0:1024 // 2].rearrange("p (k m) -> p k m", k=2)
        wgate = spare[:, 512:1024].rearrange("p (k m) -> p k m", k=2)
        wqpk = spare[0:32, 1024:2048]
        pkk = spare[0:32, 2048:3072]

        ident = sb("ident", [P, P])
        causal = sb("causal", [P, P])
        pos = sb("pos", [P, PAIRS])
        headoff = sb("headoff", [P, UNITS * TOPK])
        wkv_raw = sb("wkv_raw", [C, 2 * C])
        lnkv_s = sb("lnkv_s", [C, 2])
        wq_raw = sb("wq_raw", [C, C])
        lnq_s = sb("lnq_s", [C, 2])
        proj_raw = sb("proj_raw", [C + 1, C])
        w_in = sb("w_in", [C, 2 * INNER])
        wx_rows = sb("wx_rows", [RANK, INNER])
        wx_cols = sb("wx_cols", [INNER, RANK + 2 * STATE])
        wdt = sb("wdt", [RANK, INNER])
        bdt = sb("bdt", [INNER, 1])
        alog = sb("alog", [INNER, 2 * STATE])
        dskip = sb("dskip", [INNER, 2])
        bglob = sb("bglob", [P, 2])
        bgate = sb("bgate", [P, 2])
        wout = sb("wout", [P, 2, C])
        wq_ffn = sb("wq_ffn", [C, PK_HEADS * C])
        wo_ffn = sb("wo_ffn", [P, PK_HEADS, C])
        wkv = sb("wkv", [P, KVW])
        mean16 = sb("mean16", [C, C])
        ones64 = sb("ones64", [C, C])
        lq = sb("lq", [C, C + 1])
        wq = sb("wq", [C + 1, C + HEADS])
        kvbias = sb("kvbias", [C + 1, C])
        wq_kb = sb("wq_kb", [C + 1, C])
        lp = sb("lp", [C + 1, C + 1])
        proj = sb("proj", [C + 1, C])
        w_delta = sb("w_delta", [INNER, INNER])
        a_neg = sb("a_neg", [INNER, 2 * STATE])
        diag = sb("diag", [INNER, 2, INNER])
        w_gg = sb("w_gg", [P, 2, 2 * INNER])
        nbias_g = sb("nbias_g", [P, 2])
        w_sim = sb("w_sim", [C, 2 * PK_HEADS * KEYS])

        pix = sb("pix", [P, N * TOK])
        wide = sb("wide", [P, TILES * N * KVW])
        kv = wide[:].rearrange("p (t n w) -> p t n w", t=TILES, n=N)
        scratch = sb("scratch", [P, SCRATCH])
        rf = sb("rf", [P, TILES, C])
        st6 = sb("st6", [P, TILES, 6])
        mv = sb("mv", [P, TILES, 2])
        var = sb("var", [P, TILES * N + TILES])
        lnv = sb("lnv", [P, TILES * N + TILES])
        rstd = sb("rstd", [P, TILES * N + TILES])
        newt = sb("newt", [P, TILES * N + TILES])
        nrm = sb("nrm", [P, TILES, C])
        turned = sb("turned", [C + 1, TOK])
        qs = sb("qs", [P, TILES, C + HEADS])
        sc = sb("sc", [P, TILES * N * HEADS])
        mx = sb("mx", [P, TILES * HEADS])
        den = sb("den", [P, TILES * HEADS])
        h1 = sb("h1", [P, TILES, C])
        ez = wide[:, 0:2 * TOK]
        ez1 = wide[:, 2 * TOK:4 * TOK]
        uz = sb("uz", [INNER, 2, TOK])
        dabs = sb("dabs", [INNER, TOK])
        dlog = sb("dlog", [INNER, TOK])
        pixsum = dabs[0:C, :]
        delta = sb("delta", [INNER, TOK])
        du = sb("du", [INNER, TOK])
        decay = [sb(f"decay{k}", [INNER, STATE * TOK]) for k in range(2)]
        inject = wide[:, 0:STATE * TOK]
        yg = sb("yg", [INNER, 2, TOK])
        ysum = sb("ysum", [INNER, 2])
        ge = sb("ge", [INNER, 2])
        gate = sb("gate", [INNER, 2])
        wout_g = sb("wout_g", [INNER, 2, C])
        sim = scratch[:, 0:TILES * 2 * PK_HEADS * KEYS].rearrange("p (t j h k) -> p t j h k", t=TILES, j=2, h=PK_HEADS)
        best = sb("best", [P, 2, UNITS, TOPK])
        best_i = sb("best_i", [P, 2, UNITS, TOPK], U32)
        frac = sb("frac", [P, 2, UNITS, TOPK])
        pair = sb("pair", [P, UNITS, PAIRS])
        pair_row = sb("pair_row", [P, UNITS, PAIRS])
        fin = sb("fin", [P, UNITS, TOPK])
        fin_i = sb("fin_i", [P, UNITS, TOPK], U32)
        fin_p = sb("fin_p", [P, UNITS, TOPK])
        row_f = sb("row_f", [P, UNITS, TOPK])
        wexp = sb("wexp", [P, UNITS, TOPK])
        wden = sb("wden", [P, UNITS])
        rows = [sb(f"rows{k}", [P, UNITS * TOPK], U32) for k in range(2)]
        wts = [sb(f"wts{k}", [P, UNITS, TOPK]) for k in range(2)]
        acc = [sb(f"acc{k}", [P, TILES, C]) for k in range(2)]
        xT = [sb(f"xT{k}", [C, TOK]) for k in range(2)]
        kvT = sb("kvT", [P, 2, TOK])
        qT = sb("qT", [C, TOK])
        vo = sb("vo", [P, TILES, C])
        negmax = sb("negmax", [P, TILES])
        rowsum = sb("rowsum", [P, TILES])
        rrow = sb("rrow", [P, TILES])
        prob = sb("prob", [P, 3 * P])
        probT = sb("probT", [P, 3 * P])

        loads = sem("loads")
        w_mm = sem("w_mm")
        w_dve = sem("w_dve")
        w_act = sem("w_act")
        x_loaded = sem("x_loaded")
        x_squared = sem("x_squared")
        pixels_summed = sem("pixels_summed")
        rf_ready = sem("rf_ready")
        kv_ready = sem("kv_ready")
        kv_copied = sem("kv_copied")
        var_ready = sem("var_ready")
        rsqrt_ready = sem("rsqrt_ready")
        nrm_ready = sem("nrm_ready")
        turn_ready = sem("turn_ready")
        turn_copied = sem("turn_copied")
        q_ready = sem("q_ready")
        proj_ready = sem("proj_ready")
        scores_ready = sem("scores_ready")
        probs_ready = sem("probs_ready")
        xz_ready = sem("xz_ready")
        xz_exp = sem("xz_exp")
        uz_ready = sem("uz_ready")
        dt_ready = sem("dt_ready")
        dt_log = sem("dt_log")
        delta_ready = sem("delta_ready")
        bc_ready = sem("bc_ready")
        bc_used = sem("bc_used")
        decay_ready = sem("decay_ready")
        y_ready = sem("y_ready")
        ysum_ready = sem("ysum_ready")
        gate_mm = sem("gate_mm")
        gate_exp = sem("gate_exp")
        wout_ready = sem("wout_ready")
        block_ready = sem("block_ready")
        sim_ready = sem("sim_ready")
        sim_copied = sem("sim_copied")
        pick_ready = sem("pick_ready")
        pick_exp = sem("pick_exp")
        rows_ready = sem("rows_ready")
        wts_ready = sem("wts_ready")
        gathered = [sem(f"gathered{k}") for k in range(SLOTS)]
        weighted = sem("weighted")
        summed = sem("summed")
        kvT_copied = sem("kvT_copied")
        qT_ready = sem("qT_ready")
        qT_copied = sem("qT_copied")
        vo_ready = sem("vo_ready")
        vo_copied = sem("vo_copied")
        s_ready = sem("s_ready")
        max_ready = sem("max_ready")
        p_ready = sem("p_ready")
        pT_ready = sem("pT_ready")
        pT_copied = sem("pT_copied")
        o_ready = sem("o_ready")
        acc_ready = sem("acc_ready")
        stored = sem("stored")
        held = sem("held")
        dve_step = sem("dve_step")
        act_step = sem("act_step")


        NLOAD = 27

        block = ctx.enter_context(nc.Block())

        @block.sync
        def _(sp):
            for dst, src in (
                    (ident[:], ident_d), (causal[:], causal_d), (pos[:], pos_d), (headoff[:], headoff_d),
                    (wkv_raw[:], wkvT), (lnkv_s[:], lnkv), (wq_raw[:], wqT), (lnq_s[:], lnq),
                    (proj_raw[:], projE), (w_in[:], w_inT), (wx_rows[:], w_x[0:RANK, :]),
                    (wx_cols[:], w_xT), (wdt[:], w_dtT), (bdt[:], b_dt), (alog[:], a_log),
                    (dskip[:], d_skip), (wglob, w_global.rearrange("(k p) m -> p k m", p=P)),
                    (wgate, w_gateT.rearrange("(k p) m -> p k m", p=P)),
                    (bglob[:], b_global), (bgate[:], b_gate),
                    (wout[:], w_outT.rearrange("(k p) m -> p k m", p=P)),
                    (wqpk, wq_pkT), (pkk, pk_keysT), (wq_ffn[:], w_q),
                    (wo_ffn[C:P, :, :], w_o.rearrange("(h d) c -> d h c", d=C)),
                    (pix[0:C, :], x[0]), (pix[C:P, :], x[0])):
                sp.dma_start(dst, src).then_inc(loads, 16)

            def load_image(a):
                sp.wait_ge(kv_ready, a * NKV)
                sp.dma_start(pix[0:C, :], x[a]).then_inc(x_loaded, 16)
                sp.dma_start(pix[C:P, :], x[a]).then_inc(x_loaded, 16)

            def store_image(b, k):
                sp.wait_ge(acc_ready, b * PK_HEADS + PK_HEADS)
                sp.dma_start(out[b].rearrange("(t p) c -> p t c", p=P), acc[k][:]).then_inc(stored, 16)

            load_image(1)
            load_image(2)
            store_image(0, 0)
            with sp.Fori(0, IMAGES // 2 - 2) as i:
                load_image(i * 2 + 3)
                store_image(i * 2 + 1, 1)
                load_image(i * 2 + 4)
                store_image(i * 2 + 2, 0)
            load_image(IMAGES - 1)
            for b in range(IMAGES - 3, IMAGES):
                store_image(b, b % 2)
            sp.wait_ge(stored, 16 * IMAGES)

        @block.gpsimd
        def _(pool):
            def gather_image(b, k):
                for u in range(UNITS):
                    if u % GROUP == 0:
                        pool.wait_ge(rows_ready, b * (UNITS // GROUP) + (u // GROUP + 1))
                    if u >= SLOTS:
                        pool.wait_ge(summed, b * UNITS + (u - SLOTS + 1))
                    elif not (isinstance(b, int) and b == 0):
                        pool.wait_ge(summed, b * UNITS + (u - SLOTS + 1))
                    pool.sem_inc(held, 1)
                    for j in range(TOPK):
                        pool.indirect_dma_start(
                            out=gath[:, u % SLOTS, j, :], out_offset=None, in_=table,
                            in_offset=bass.IndirectOffsetOnAxis(
                                ap=rows[k][:, u * TOPK + j:u * TOPK + j + 1], axis=0),
                        ).then_inc(gathered[u % SLOTS], 16)

            gather_image(0, 0)
            with pool.Fori(0, IMAGES // 2 - 1) as i:
                gather_image(i * 2 + 1, 1)
                gather_image(i * 2 + 2, 0)
            gather_image(IMAGES - 1, 1)

        @block.tensor
        def _(pe):
            mm = nc.tensor.matmul

            def prepare():
                pe.wait_ge(w_dve, 1)
                mm(small_ps[0:C, 0:2 * C], ones64[:], wkv[0:C, 0:2 * C], start=True, stop=True)
                mm(small_ps[0:C + 1, 128:192], lnkv_s[:, 1:2].to_broadcast([C, C + 1]), wkv_raw[:, 0:C],
                   start=True, stop=True)
                mm(small_ps[0:C, 192:193], wkv_raw[:, C:2 * C], lnkv_s[:, 1:2], start=True, stop=True)
                mm(small_ps[0:C + 1, 256:320], lq[:], wq_raw[:], start=True, stop=True)
                mm(small_ps[:, 320:448], wx_rows[:], wdt[:], start=True, stop=True).then_inc(w_mm, 1)
                for k in range(2):
                    for j in range(2):
                        mm(scan_ps[:, k * 256:(k + 1) * 256], wglob[:, j, k * P:(k + 1) * P], wgate[:, j, :],
                           start=(j == 0), stop=(j == 1))
                for m in range(2):
                    for j in range(2):
                        mm(turn_ps[:, m:m + 1], wgate[:, j, m * P:(m + 1) * P], bglob[:, j:j + 1],
                           start=(j == 0), stop=(j == 1))
                for g in range(2 * PK_HEADS):
                    last = mm(big_ps[g // 8][0:C, g % 8 * KEYS:(g % 8 + 1) * KEYS],
                              wqpk[:, g * C:(g + 1) * C], pkk[:, g * KEYS:(g + 1) * KEYS],
                              start=True, stop=True)
                last.then_inc(w_mm, 1)
                pe.wait_ge(w_dve, 2)
                pe.wait_ge(w_act, 2)
                mm(small_ps[0:C + 1, 448:512], lp[:], proj_raw[:], start=True, stop=True).then_inc(w_mm, 1)
                pe.wait_ge(w_dve, 3)

            def turn(a, n):
                pe.wait_ge(nrm_ready, a * 4 + (n + 1))
                pe.sem_inc(held, 1)
                for t in range(TILES):
                    last = pe.transpose(turn_ps[0:C, t * P:(t + 1) * P], nrm[:, t, :], ident[:])
                last.then_inc(turn_ready, 1)

            def add_states(c):
                for n in (2 * c, 2 * c + 1):
                    for r in range(2):
                        mm(scan_ps[:, r * TOK:(r + 1) * TOK], ident[:], decay[r][:, n * TOK:(n + 1) * TOK],
                           start=(n == 0 and r == 0), stop=False, skip_group_check=True)

            def front(a, k, s):
                first = isinstance(a, int) and a == 0
                if s == 0 and not first:
                    pe.wait_ge(x_loaded, a * 32)
                if s == 0:
                    pe.sem_inc(held, 1)
                if s in (0, 1):
                    t = s
                    if s == 0:
                        pe.wait_ge(x_squared, a * 1 + 1)
                    for j, (n0, w) in enumerate(KV_CHUNKS):
                        c = t * len(KV_CHUNKS) + j
                        if c >= 2:
                            pe.wait_ge(kv_copied, a * NKV + (c - 1))
                        elif not first:
                            pe.wait_ge(sim_copied, a * 4)
                        for n in range(n0, n0 + w):
                            last = mm(big_ps[c % 2][:, (n - n0) * KVW:(n - n0 + 1) * KVW],
                                      pix[:, n * TOK + t * P:n * TOK + (t + 1) * P], wkv[:],
                                      start=True, stop=True)
                        last.then_inc(kv_ready, 1)
                if s == 0:
                    pe.wait_ge(pixels_summed, a * 1 + 1)
                    for t in range(TILES):
                        last = mm(small_ps[:, t * C:(t + 1) * C], pixsum[:, t * P:(t + 1) * P], mean16[:],
                                  start=True, stop=True)
                    last.then_inc(rf_ready, 1)
                if s == 2:
                    turn(a, 0)
                    pe.wait_ge(turn_copied, a * 4 + 1)
                    for t in range(TILES):
                        last = mm(small_ps[:, 128 + t * 72:200 + t * 72], turned[:, t * P:(t + 1) * P], wq[:],
                                  start=True, stop=True)
                    last.then_inc(q_ready, 1)
                if s == 3:
                    turn(a, 1)
                    pe.wait_ge(turn_copied, a * 4 + 2)
                    for t in range(TILES):
                        last = mm(small_ps[:, 272 + t * C:272 + (t + 1) * C], turned[:, t * P:(t + 1) * P],
                                  proj[:], start=True, stop=True)
                    last.then_inc(proj_ready, 1)
                if s == 4:
                    turn(a, 2)
                    pe.wait_ge(turn_copied, a * 4 + 3)
                    for j in range(2):
                        last = mm(scan_ps[:, j * TOK:(j + 1) * TOK], w_in[:, j * INNER:(j + 1) * INNER],
                                  turned[0:C, :], start=True, stop=True)
                    last.then_inc(xz_ready, 1)
                    pe.wait_ge(uz_ready, a * 1 + 1)
                    mm(scan_ps[:, 0:TOK], w_delta[:], uz[:, 0, :], start=True, stop=True).then_inc(dt_ready, 1)
                if s in (5, 7):
                    for c in range(NBC + (2 if s == 7 else 0)):
                        m = c + (NBC if s == 7 else 0)
                        if m >= 2:
                            pe.wait_ge(bc_used, a * 2 * NBC + (m - 1))
                        if s == 7 and c >= 2:
                            add_states(c - 2)
                        if c >= NBC:
                            continue
                        for j in range(2):
                            n = 2 * c + j
                            col = RANK + n + (STATE if s == 7 else 0)
                            last = mm(big_ps[m % 2][:, j * TOK:(j + 1) * TOK],
                                      wx_cols[:, col:col + 1].to_broadcast([INNER, INNER]), uz[:, 0, :],
                                      start=True, stop=True)
                        last.then_inc(bc_ready, 1)
                if s == 7:
                    for r in range(2):
                        last = mm(scan_ps[:, r * TOK:(r + 1) * TOK], diag[:, r, :], uz[:, 0, :],
                                  start=False, stop=True, skip_group_check=True)
                    last.then_inc(y_ready, 1)
                if s == 9:
                    pe.wait_ge(ysum_ready, a * 1 + 1)
                    for m in range(2):
                        for j in range(2):
                            last = mm(turn_ps[:, 384 + m:385 + m], w_gg[:, j, m * P:(m + 1) * P],
                                      ysum[:, j:j + 1], start=(j == 0), stop=(j == 1))
                    last.then_inc(gate_mm, 1)
                    pe.wait_ge(wout_ready, a * 1 + 1)
                    for t in range(TILES):
                        for j in range(2):
                            last = mm(turn_ps[:, 256 + t * C:256 + (t + 1) * C], yg[:, j, t * P:(t + 1) * P],
                                      wout_g[:, j, :], start=(j == 0), stop=(j == 1))
                    last.then_inc(block_ready, 1)
                if s == 10:
                    turn(a, 3)
                    pe.wait_ge(turn_copied, a * 4 + 4)
                    for t in range(TILES):
                        for j in range(2):
                            if t > 0:
                                pe.wait_ge(sim_copied, a * 4 + (j + 1))
                            mm(big_ps[j][:], xT[k][:, t * P:(t + 1) * P], w_sim[:, j * 512:(j + 1) * 512],
                               start=True, stop=True).then_inc(sim_ready, 1)

            def unit(b, k, u):
                pe.wait_ge(weighted, b * UNITS + (u + 1))
                if u >= 1 or not (isinstance(b, int) and b == 0):
                    pe.wait_ge(kvT_copied, b * UNITS + u)
                q = u % 4
                for j in range(TOPK):
                    last = mm(sum_ps[:, q * P:(q + 1) * P], gath[:, u % SLOTS, j, :], ident[:],
                              start=(j == 0), stop=(j == TOPK - 1))
                last.then_inc(summed, 1)

            def scores(b, k, h):
                started = h > 0 or not (isinstance(b, int) and b == 0)
                n = b * PK_HEADS + h
                kvh = kvT[:, h % 2, :]
                if started:
                    pe.wait_ge(acc_ready, n)
                pe.sem_inc(held, 1)
                mm(prob_ps[0:C, 0:TOK], wq_ffn[:, h * C:(h + 1) * C], xT[k][:],
                   start=True, stop=True).then_inc(qT_ready, 1)
                pe.wait_ge(kvT_copied, b * UNITS + (2 * h + 2))
                for t in range(TILES):
                    last = mm(score_ps[:, 384 + t * C:384 + (t + 1) * C], kvh[C:P, t * P:(t + 1) * P],
                              wo_ffn[C:P, h, :], start=True, stop=True)
                last.then_inc(vo_ready, 1)
                pe.wait_ge(qT_copied, n + 1)
                pe.wait_ge(vo_copied, n + 1)
                mm(score_ps[:, 0:P], qT[:, 0:P], kvh[0:C, 0:P], start=True, stop=False)
                mm(score_ps[:, 0:P], ident[:], causal[:], start=False, stop=True)
                mm(score_ps[:, P:3 * P], qT[:, P:TOK], kvh[0:C, :], start=True, stop=False)
                mm(score_ps[:, 2 * P:3 * P], ident[:], causal[:], start=False, stop=True).then_inc(s_ready, 1)

            def turn_probs(b, h):
                pe.wait_ge(p_ready, b * PK_HEADS + (h + 1))
                pe.sem_inc(held, 1)
                for j in range(3):
                    last = pe.transpose(prob_ps[:, j * P:(j + 1) * P], prob[:, j * P:(j + 1) * P], ident[:])
                last.then_inc(pT_ready, 1)

            def output(b, h):
                pe.wait_ge(pT_copied, b * PK_HEADS + (h + 1))
                mm(prob_ps[:, 384:448], probT[:, 0:P], vo[:, 0, :], start=True, stop=True)
                mm(prob_ps[:, 448:512], probT[:, P:2 * P], vo[:, 0, :], start=True, stop=False)
                mm(prob_ps[:, 448:512], probT[:, 2 * P:3 * P], vo[:, 1, :],
                   start=False, stop=True).then_inc(o_ready, 1)

            def image(b, k, left):
                for u in range(UNITS):
                    for what, n in steps(u, left):
                        if what == "front":
                            front(b + n[0], (k + n[0]) % 2, n[1])
                        if what == "sum":
                            unit(b, k, n)
                        if what == "scores":
                            scores(b, k, n)
                        if what == "turn":
                            turn_probs(b, n)
                        if what == "add":
                            output(b, n)

            prepare()
            for s in range(PIECES):
                front(0, 0, s)
                if s == 12:
                    front(1, 1, 0)
                if s == 14:
                    front(1, 1, 1)
            image(0, 0, 2)
            with pe.Fori(0, IMAGES // 2 - 2) as i:
                image(i * 2 + 1, 1, 2)
                image(i * 2 + 2, 0, 2)
            image(IMAGES - 3, 1, 2)
            image(IMAGES - 2, 0, 1)
            image(IMAGES - 1, 1, 0)

        @block.scalar
        def _(act):
            af = nc.scalar.activation
            count = [0]

            def step(ins):
                count[0] += 1
                return ins.then_inc(act_step, 1)

            def settle():
                act.wait_ge(act_step, count[0])

            def prepare():
                act.wait_ge(loads, 16 * NLOAD)
                af(a_neg[:], alog[:], ACT.Exp).then_inc(w_act, 1)
                act.wait_ge(w_dve, 2)
                af(w_delta[:], small_ps[:, 320:448], ACT.Copy).then_inc(w_act, 1)
                act.wait_ge(w_mm, 2)
                af(w_gg[:].rearrange("p k m -> p (k m)"), scan_ps[:], ACT.Copy).then_inc(w_act, 1)
                for j in range(2):
                    af(w_sim[:, j * 512:(j + 1) * 512], big_ps[j][0:C, :], ACT.Copy).then_inc(w_act, 1)

            def turn_copy(a, n, dst):
                act.wait_ge(turn_ready, a * 4 + (n + 1))
                af(dst, turn_ps[0:C, 0:TOK], ACT.Copy).then_inc(turn_copied, 1)

            def rsqrt(a, n, w):
                act.wait_ge(var_ready, a * 3 + (n + 1))
                step(af(lnv[:, 0:w], var[:, 0:w], ACT.Ln))
                settle()
                af(rstd[:, 0:w], lnv[:, 0:w], ACT.Exp, scale=-0.5).then_inc(rsqrt_ready, 1)

            def front(a, k, s):
                first = isinstance(a, int) and a == 0
                if s == 0:
                    if not first:
                        act.wait_ge(x_loaded, a * 32)
                    af(pix[C:P, :], pix[C:P, :], ACT.Square).then_inc(x_squared, 1)
                if s in (0, 1):
                    for j, (n0, w) in enumerate(KV_CHUNKS):
                        c = s * len(KV_CHUNKS) + j
                        act.wait_ge(kv_ready, a * NKV + (c + 1))
                        af(kv[:, s, n0:n0 + w, :].rearrange("p n w -> p (n w)"), big_ps[c % 2][:, 0:w * KVW],
                           ACT.Copy).then_inc(kv_copied, 1)
                if s == 1:
                    rsqrt(a, 0, TILES * N + TILES)
                if s == 2:
                    turn_copy(a, 0, turned[0:C, :])
                    act.wait_ge(scores_ready, a * 1 + 1)
                    af(sc[:], sc[:], ACT.Exp, scale=C ** -0.5).then_inc(probs_ready, 1)
                if s == 3:
                    turn_copy(a, 1, turned[0:C, :])
                    rsqrt(a, 1, TILES)
                if s == 4:
                    turn_copy(a, 2, turned[0:C, :])
                    act.wait_ge(xz_ready, a * 1 + 1)
                    af(ez, scan_ps[:], ACT.Exp, scale=-1.0).then_inc(xz_exp, 1)
                    act.wait_ge(dt_ready, a * 1 + 1)
                    step(af(dabs[:], scan_ps[:, 0:TOK], ACT.Abs, bias=bdt[:, 0:1]))
                    settle()
                    step(af(dlog[:], dabs[:], ACT.Exp, scale=-1.0))
                    settle()
                    af(dlog[:], dlog[:], ACT.Ln, bias=1.0).then_inc(dt_log, 1)
                if s == 5:
                    act.wait_ge(delta_ready, a * 1 + 1)
                    for r in range(2):
                        for n in range(STATE):
                            last = af(decay[r][:, n * TOK + 1 - r:(n + 1) * TOK - r], delta[:, 1 - r:TOK - r],
                                      ACT.Exp, scale=a_neg[:, r * STATE + n:r * STATE + n + 1])
                        last.then_inc(decay_ready, 1)
                if s == 9:
                    act.wait_ge(gate_mm, a * 1 + 1)
                    for m in range(2):
                        last = af(ge[:, m:m + 1], turn_ps[:, 384 + m:385 + m], ACT.Exp, scale=-1.0 / TOK,
                                  bias=nbias_g[:, m:m + 1])
                    last.then_inc(gate_exp, 1)
                    rsqrt(a, 2, TILES)
                if s == 10:
                    turn_copy(a, 3, xT[k][:])
                    for t in range(TILES):
                        for j in range(2):
                            act.wait_ge(sim_ready, a * 4 + (2 * t + j + 1))
                            af(sim[:, t, j, :, :].rearrange("p h k -> p (h k)"), big_ps[j][:],
                               ACT.Copy).then_inc(sim_copied, 1)
                if s == 14:
                    act.wait_ge(pick_ready, a * 1 + 1)
                    af(wexp[:], wexp[:], ACT.Exp).then_inc(pick_exp, 1)

            def weigh(b, k, u):
                act.wait_ge(gathered[u % SLOTS], b * (UNITS // SLOTS * TOPK * 16) + (u // SLOTS + 1) * TOPK * 16)
                act.wait_ge(wts_ready, b + 1)
                if u:
                    act.wait_ge(weighted, b * UNITS + u)
                for j in range(TOPK):
                    last = af(gath[:, u % SLOTS, j, :], gath[:, u % SLOTS, j, :], ACT.Copy,
                              scale=wts[k][:, u, j:j + 1])
                last.then_inc(weighted, 1)

            def unit(b, u):
                act.wait_ge(summed, b * UNITS + (u + 1))
                if u >= 4 or not (isinstance(b, int) and b == 0):
                    act.wait_ge(s_ready, b * PK_HEADS + (u // 2 - 1))
                af(kvT[:, u // 2 % 2, u % 2 * P:(u % 2 + 1) * P], sum_ps[:, u % 4 * P:(u % 4 + 1) * P],
                   ACT.Copy).then_inc(kvT_copied, 1)

            def scores(b, h):
                n = b * PK_HEADS + h
                act.wait_ge(qT_ready, n + 1)
                af(qT[:], prob_ps[0:C, 0:TOK], ACT.Copy, scale=C ** -0.5).then_inc(qT_copied, 1)
                act.wait_ge(vo_ready, n + 1)
                af(vo[:].rearrange("p t c -> p (t c)"), score_ps[:, 384:512], ACT.Copy).then_inc(vo_copied, 1)

            def exponentials(b, h):
                n = b * PK_HEADS + h
                act.wait_ge(max_ready, n + 1)
                af(prob[:, 0:P], score_ps[:, 0:P], ACT.Exp, bias=negmax[:, 0:1], accum_out=rowsum[:, 0:1])
                af(prob[:, P:3 * P], score_ps[:, P:3 * P], ACT.Exp, bias=negmax[:, 1:2],
                   accum_out=rowsum[:, 1:2]).then_inc(p_ready, 1)

            def turn_probs(b, h):
                act.wait_ge(pT_ready, b * PK_HEADS + (h + 1))
                af(probT[:], prob_ps[:, 0:3 * P], ACT.Copy).then_inc(pT_copied, 1)

            def new_image():
                settle()
                act.sem_clear(act_step)
                count[0] = 0

            def image(b, k, left):
                if left:
                    new_image()
                for u in range(UNITS):
                    for what, n in steps(u, left):
                        if what == "front":
                            front(b + n[0], (k + n[0]) % 2, n[1])
                        if what == "sum":
                            unit(b, n)
                        if what == "weigh" and n in ON_ACT:
                            weigh(b, k, n)
                        if what == "scores":
                            scores(b, n)
                        if what == "max":
                            exponentials(b, n)
                        if what == "turn":
                            turn_probs(b, n)

            act.preload_act_table_set("natural_log_exp_and_others")
            prepare()
            for s in range(PIECES):
                front(0, 0, s)
                if s == 12:
                    front(1, 1, 0)
                if s == 14:
                    front(1, 1, 1)
            image(0, 0, 2)
            with act.Fori(0, IMAGES // 2 - 2) as i:
                image(i * 2 + 1, 1, 2)
                image(i * 2 + 2, 0, 2)
            image(IMAGES - 3, 1, 2)
            image(IMAGES - 2, 0, 1)
            image(IMAGES - 1, 1, 0)

        @block.vector
        def _(dve):
            v = nc.vector
            count = [0]

            told = [None]

            def step(ins, sem=None, value=0):
                if sem is None:
                    count[0] += 1
                    told[0] = None
                    return ins.then_inc(dve_step, 1)
                told[0] = (sem, value)
                return ins.then_inc(sem, 1)

            def settle():
                if told[0]:
                    dve.wait_ge(*told[0])
                    told[0] = None
                    alone()
                else:
                    dve.wait_ge(dve_step, count[0])

            def alone():
                dve.sem_inc(held, 1)

            def prepare():
                dve.wait_ge(loads, 16 * NLOAD)
                step(v.memset(wkv[:], 0.0))
                step(v.memset(turned[C:C + 1, :], 1.0))
                step(v.memset(ones64[:], 1.0 / C))
                step(v.tensor_scalar(mean16[:], ident[0:C, 0:C], 1.0 / N, None, ALU.mult))
                step(v.tensor_scalar(lq[:, 0:C], ident[0:C, 0:C], lnq_s[:, 0:1], None, ALU.mult))
                step(v.tensor_copy(lq[:, C:C + 1], lnq_s[:, 1:2]))
                step(v.tensor_copy(lp[:], ident[0:C + 1, 0:C + 1]))
                for r in range(2):
                    step(v.tensor_scalar(diag[:, r, :], ident[:], dskip[:, r:r + 1], None, ALU.mult))
                settle()
                step(v.memset(wkv[C:P, 2 * C:2 * C + 1], 1.0 / C))
                step(v.memset(wkv[0:C, 2 * C + 1:2 * C + 2], 1.0 / C))
                step(v.tensor_scalar(wkv[0:C, 0:2 * C], wkv_raw[:], lnkv_s[:, 0:1], None, ALU.mult))
                settle()
                step(v.tensor_copy(ysum[:], dskip[:]), w_dve, 1)
                dve.wait_ge(w_act, 1)
                step(v.tensor_scalar(a_neg[:], a_neg[:], -1.0, None, ALU.mult))
                dve.wait_ge(w_mm, 1)
                step(v.tensor_tensor(wkv[0:C, 0:2 * C], wkv[0:C, 0:2 * C], small_ps[0:C, 0:2 * C], ALU.subtract))
                step(v.tensor_copy(kvbias[:], small_ps[0:C + 1, 128:192]))
                step(v.tensor_copy(wq[:, 0:C], small_ps[0:C + 1, 256:320]))
                step(v.tensor_copy(lp[0:C, C:C + 1], small_ps[0:C, 192:193]))
                settle()
                step(v.tensor_tensor(wq_kb[:], wq[:, 0:C], kvbias[:], ALU.mult), w_dve, 2)
                settle()
                step(v.tensor_reduce(wq[:, C:C + HEADS], wq_kb[:].rearrange("p (h d) -> p h d", d=D), AX, ALU.add))
                dve.wait_ge(w_mm, 2)
                step(v.tensor_tensor(nbias_g[:], turn_ps[:, 0:2], bgate[:], ALU.add))
                settle()
                step(v.tensor_scalar(nbias_g[:], nbias_g[:], -1.0, None, ALU.mult))
                dve.wait_ge(w_mm, 3)
                dve.wait_ge(w_act, 5)
                step(v.tensor_copy(proj[:], small_ps[0:C + 1, 448:512]))
                settle()
                step(v.tensor_copy(mx[:, 0:2], dskip[:]), w_dve, 3)
                settle()

            def newton(a, n, w):
                dve.wait_ge(rsqrt_ready, a * 3 + (n + 1))
                step(v.scalar_tensor_tensor(newt[:, 0:w], rstd[:, 0:w], -0.5, rstd[:, 0:w], ALU.mult, ALU.mult))
                settle()
                step(v.tensor_tensor(newt[:, 0:w], newt[:, 0:w], var[:, 0:w], ALU.mult))
                settle()
                step(v.scalar_tensor_tensor(rstd[:, 0:w], newt[:, 0:w], 1.5, rstd[:, 0:w], ALU.add, ALU.mult))
                settle()

            def moments(src, at, *signal):
                for t in range(TILES):
                    step(v.bn_stats(st6[:, t, :], src[t]))
                settle()
                for t in range(TILES):
                    step(v.bn_aggr(mv[:, t, :], st6[:, t, :]))
                settle()
                ins = v.tensor_scalar(var[:, at:at + TILES], mv[:, :, 1], EPS, None, ALU.add)
                step(ins, *signal)

            def normalize(src, at, value):
                for t in range(TILES):
                    last = v.tensor_scalar(nrm[:, t, :], src[t], mv[:, t, 0:1], rstd[:, at + t:at + t + 1],
                                           ALU.subtract, ALU.mult)
                step(last, nrm_ready, value)

            def front(a, k, s):
                first = isinstance(a, int) and a == 0
                nt = TILES * N
                if s == 0:
                    if not (isinstance(a, int) and a == 0):
                        dve.wait_ge(x_loaded, a * 32)
                    step(v.tensor_reduce(pixsum, pix[0:C, :].rearrange("p (n l) -> p l n", n=N), AX, ALU.add),
                         pixels_summed, a + 1)
                if s == 1:
                    dve.wait_ge(rf_ready, a * 1 + 1)
                    step(v.tensor_copy(rf[:].rearrange("p t c -> p (t c)"), small_ps[:, 0:TILES * C]))
                    settle()
                    moments([rf[:, t, :] for t in range(TILES)], nt)
                    dve.wait_ge(kv_copied, a * NKV + NKV)
                    kvf = wide[:].rearrange("p (m w) -> p m w", w=KVW)
                    step(v.tensor_tensor(newt[:, 0:nt], kvf[:, :, 2 * C + 1], kvf[:, :, 2 * C + 1], ALU.mult))
                    settle()
                    step(v.scalar_tensor_tensor(var[:, 0:nt], kvf[:, :, 2 * C], EPS, newt[:, 0:nt],
                                                ALU.add, ALU.subtract), var_ready, a * 3 + 1)
                    newton(a, 0, nt + TILES)
                    normalize([rf[:, t, :] for t in range(TILES)], nt, a * 4 + 1)
                if s == 2:
                    dve.wait_ge(q_ready, a * 1 + 1)
                    step(v.tensor_copy(qs[:].rearrange("p t c -> p (t c)"), small_ps[:, 128:272]))
                    settle()
                    prod = scratch[:, 0:nt * C].rearrange("p (t n c) -> p t n c", t=TILES, n=N)
                    step(v.tensor_tensor(prod, kv[:, :, :, 0:C],
                                         qs[:, :, 0:C].unsqueeze(2).to_broadcast([P, TILES, N, C]), ALU.mult))
                    settle()
                    step(v.tensor_reduce(sc[:], scratch[:, 0:nt * C].rearrange("p (m d) -> p m d", d=D), AX, ALU.add))
                    settle()
                    sc3 = sc[:].rearrange("p (m h) -> p m h", h=HEADS)
                    sc4 = sc[:].rearrange("p (t n h) -> p t n h", t=TILES, h=HEADS)
                    rs3 = rstd[:, 0:nt].unsqueeze(2).to_broadcast([P, nt, HEADS])
                    step(v.tensor_tensor(sc3, sc3, rs3, ALU.mult))
                    settle()
                    step(v.tensor_tensor(sc4, sc4, qs[:, :, C:].unsqueeze(2).to_broadcast([P, TILES, N, HEADS]),
                                         ALU.add))
                    settle()
                    by_n = sc[:].rearrange("p (t n h) -> p t h n", t=TILES, h=HEADS)
                    mx3 = mx[:].rearrange("p (t h) -> p t h", t=TILES)
                    den3 = den[:].rearrange("p (t h) -> p t h", t=TILES)
                    step(v.tensor_reduce(mx3, by_n, AX, ALU.max))
                    settle()
                    step(v.tensor_tensor(sc4, sc4, mx3.unsqueeze(2).to_broadcast([P, TILES, N, HEADS]),
                                         ALU.subtract), scores_ready, a + 1)
                    dve.wait_ge(probs_ready, a * 1 + 1)
                    step(v.tensor_reduce(den3, by_n, AX, ALU.add))
                    settle()
                    step(v.reciprocal(den[:], den[:]))
                    step(v.tensor_tensor(sc3, sc3, rs3, ALU.mult))
                    settle()
                    step(v.tensor_tensor(scratch[:, 0:nt * C].rearrange("p (m h d) -> p m h d", h=HEADS, d=D),
                                         wide[:].rearrange("p (m w) -> p m w", w=KVW)[:, :, C:2 * C]
                                         .rearrange("p m (h d) -> p m h d", d=D),
                                         sc3.unsqueeze(3).to_broadcast([P, nt, HEADS, D]), ALU.mult))
                    settle()
                    step(v.tensor_reduce(nrm[:], scratch[:, 0:nt * C].rearrange("p (t n c) -> p t c n", t=TILES, n=N),
                                         AX, ALU.add))
                    settle()
                    nh = nrm[:].rearrange("p t (h d) -> p (t h) d", d=D)
                    step(v.tensor_tensor(nh, nh, den[:].unsqueeze(2).to_broadcast([P, TILES * HEADS, D]),
                                         ALU.mult), nrm_ready, a * 4 + 2)
                if s == 3:
                    dve.wait_ge(proj_ready, a * 1 + 1)
                    step(v.tensor_tensor(h1[:].rearrange("p t c -> p (t c)"), small_ps[:, 272:400],
                                         rf[:].rearrange("p t c -> p (t c)"), ALU.add))
                    settle()
                    moments([h1[:, t, :] for t in range(TILES)], 0, var_ready, a * 3 + 2)
                    newton(a, 1, TILES)
                    normalize([h1[:, t, :] for t in range(TILES)], 0, a * 4 + 3)
                if s == 4:
                    dve.wait_ge(xz_exp, a * 1 + 1)
                    step(v.tensor_scalar(ez1, ez, 1.0, None, ALU.add))
                    settle()
                    step(v.reciprocal(ez1, ez1))
                    settle()
                    step(v.tensor_tensor(uz[:].rearrange("p j l -> p (j l)"), scan_ps[:], ez1,
                                         ALU.mult), uz_ready, a + 1)
                    for r in range(2):
                        first_col = decay[r][:].rearrange("p (n l) -> p n l", l=TOK)
                        step(v.memset(first_col[:, :, 0 if r == 0 else TOK - 1], 0.0))
                    dve.wait_ge(dt_ready, a * 1 + 1)
                    dve.wait_ge(dt_log, a * 1 + 1)
                    step(v.tensor_scalar(delta[:], scan_ps[:, 0:TOK], bdt[:, 0:1], 0.0, ALU.add, ALU.max))
                    settle()
                    step(v.tensor_tensor(delta[:], delta[:], dlog[:], ALU.add), delta_ready, a + 1)
                    settle()
                    step(v.tensor_tensor(du[:], delta[:], uz[:, 0, :], ALU.mult))
                    settle()
                if s == 5:
                    for c in range(NBC):
                        dve.wait_ge(bc_ready, a * 2 * NBC + (c + 1))
                        step(v.tensor_tensor(inject[:, c * 512:(c + 1) * 512].rearrange("p (j l) -> p j l", j=2),
                                             big_ps[c % 2][:].rearrange("p (j l) -> p j l", j=2),
                                             du[:].unsqueeze(1).to_broadcast([INNER, 2, TOK]),
                                             ALU.mult), bc_used, a * 2 * NBC + (c + 1))
                if s == 6:
                    settle()
                    dve.wait_ge(decay_ready, a * 2 + 1)
                    step(v.tensor_tensor_scan(decay[0][:], decay[0][:], inject, 0.0, ALU.mult, ALU.add))
                    dve.wait_ge(decay_ready, a * 2 + 2)
                    step(v.tensor_tensor_scan(decay[1][:, ::-1], decay[1][:, ::-1], inject[:, ::-1], 0.0,
                                              ALU.mult, ALU.add))
                if s == 7:
                    settle()
                    for c in range(NBC):
                        m = NBC + c
                        dve.wait_ge(bc_ready, a * 2 * NBC + (m + 1))
                        for r in range(2):
                            hs = decay[r][:, c * 512:(c + 1) * 512]
                            last = v.tensor_tensor(hs, hs, big_ps[m % 2][:], ALU.mult)
                        step(last, bc_used, a * 2 * NBC + (m + 1))
                if s == 9:
                    dve.wait_ge(y_ready, a * 1 + 1)
                    step(v.tensor_tensor(yg[:], scan_ps[:].rearrange("p (r l) -> p r l", r=2),
                                         uz[:, 1, :].unsqueeze(1).to_broadcast([INNER, 2, TOK]), ALU.mult))
                    settle()
                    step(v.tensor_reduce(ysum[:], yg[:], AX, ALU.add), ysum_ready, a + 1)
                    dve.wait_ge(gate_exp, a * 1 + 1)
                    step(v.tensor_scalar(gate[:], ge[:], 1.0, None, ALU.add))
                    settle()
                    step(v.reciprocal(gate[:], gate[:]))
                    settle()
                    for j in range(2):
                        last = v.tensor_scalar(wout_g[:, j, :], wout[:, j, :], gate[:, j:j + 1], None, ALU.mult)
                    step(last, wout_ready, a + 1)
                    dve.wait_ge(block_ready, a * 1 + 1)
                    if isinstance(a, int) and a < 2:
                        pass
                    else:
                        dve.wait_ge(stored, (a - 1) * 16)
                    settle()
                    step(v.tensor_tensor(acc[k][:].rearrange("p t c -> p (t c)"), turn_ps[:, 256:384],
                                         h1[:].rearrange("p t c -> p (t c)"), ALU.add))
                    settle()
                    moments([acc[k][:, t, :] for t in range(TILES)], 0, var_ready, a * 3 + 3)
                    newton(a, 2, TILES)
                    normalize([acc[k][:, t, :] for t in range(TILES)], 0, a * 4 + 4)
                if s in (11, 12):
                    t = s - 11
                    settle()
                    dve.wait_ge(sim_copied, a * 4 + 2 * (t + 1))
                    alone()
                    lists = [(sim[:, t, j, h, :], best[:, j, h * TILES + t, :], best_i[:, j, h * TILES + t, :])
                             for j in range(2) for h in range(PK_HEADS)]
                    top16(lists)
                if s == 13:
                    settle()
                    step(v.tensor_scalar(frac[:, 0], best_i[:, 0], FRAC, None, ALU.mult))
                    step(v.tensor_scalar(frac[:, 1], best_i[:, 1], FRAC * KEYS, None, ALU.mult))
                    for r0, rw, cw, p0 in STAIRS:
                        dst = pair[:, :, p0:p0 + rw * cw].rearrange("p u (r c) -> p u r c", c=cw)
                        step(v.tensor_tensor(dst, best[:, 0, :, r0:r0 + rw].unsqueeze(3).to_broadcast([P, UNITS, rw, cw]),
                                             best[:, 1, :, 0:cw].unsqueeze(2).to_broadcast([P, UNITS, rw, cw]), ALU.add))
                    settle()
                    for r0, rw, cw, p0 in STAIRS:
                        dst = pair_row[:, :, p0:p0 + rw * cw].rearrange("p u (r c) -> p u r c", c=cw)
                        step(v.tensor_tensor(dst, frac[:, 0, :, r0:r0 + rw].unsqueeze(3).to_broadcast([P, UNITS, rw, cw]),
                                             frac[:, 1, :, 0:cw].unsqueeze(2).to_broadcast([P, UNITS, rw, cw]), ALU.add))
                    settle()
                    step(v.tensor_tensor(pair_row[:], pair_row[:],
                                         pos[:].unsqueeze(1).to_broadcast([P, UNITS, PAIRS]), ALU.add))
                    top16([(pair[:, u, :], fin[:, u, :], fin_i[:, u, :]) for u in range(UNITS)])
                if s == 14:
                    settle()
                    step(v.tensor_copy(fin_p[:], fin_i[:]))
                    step(v.tensor_tensor(wexp[:], fin[:], fin[:, :, 0:1].to_broadcast([P, UNITS, TOPK]),
                                         ALU.subtract), pick_ready, a + 1)
                    settle()
                if s >= 14:
                    u = (s - 14) * GROUP
                    d4 = scratch[:].rearrange("p (u j e) -> p u j e", u=GROUP, j=TOPK)
                    step(v.tensor_tensor(d4, pair_row[:, u:u + GROUP, :].unsqueeze(2).to_broadcast([P, GROUP, TOPK, PAIRS]),
                                         fin_p[:, u:u + GROUP, :].unsqueeze(3).to_broadcast([P, GROUP, TOPK, PAIRS]),
                                         ALU.subtract))
                    settle()
                    step(v.tensor_reduce(row_f[:, u:u + GROUP, :], d4, AX, ALU.min, apply_absolute_value=True))
                    settle()
                    part = slice(u * TOPK, (u + GROUP) * TOPK)
                    step(v.scalar_tensor_tensor(rows[k][:, part], row_f[:, u:u + GROUP, :].rearrange("p u j -> p (u j)"),
                                                1.0 / FRAC, headoff[:, part], ALU.mult, ALU.add),
                         rows_ready, a * (UNITS // GROUP) + (s - 13))
                if s == 17:
                    dve.wait_ge(pick_exp, a * 1 + 1)
                    step(v.tensor_reduce(wden[:], wexp[:], AX, ALU.add))
                    settle()
                    step(v.reciprocal(wden[:], wden[:]))
                    settle()
                    step(v.tensor_tensor(wts[k][:], wexp[:], wden[:].unsqueeze(2).to_broadcast([P, UNITS, TOPK]),
                                         ALU.mult), wts_ready, a + 1)

            def top16(lists):
                for vals, top, idx in lists:
                    step(v.max(top[:, 0:8], vals))
                settle()
                for vals, top, idx in lists:
                    step(v.max_index(idx[:, 0:8], top[:, 0:8], vals))
                settle()
                for vals, top, idx in lists:
                    step(v.match_replace(vals, top[:, 0:8], vals, -3.0e38))
                settle()
                for vals, top, idx in lists:
                    step(v.max(top[:, 8:16], vals))
                settle()
                for vals, top, idx in lists:
                    step(v.max_index(idx[:, 8:16], top[:, 8:16], vals))

            def unit(b, k, u):
                dve.wait_ge(gathered[u % SLOTS], b * (UNITS // SLOTS * TOPK * 16) + (u // SLOTS + 1) * TOPK * 16)
                settle()
                if u:
                    dve.wait_ge(weighted, b * UNITS + u)
                g = gath[:, u % SLOTS, :, :]
                step(v.tensor_tensor(g, g, wts[k][:, u, :].unsqueeze(2).to_broadcast([P, TOPK, 2 * C]), ALU.mult),
                     weighted, b * UNITS + (u + 1))

            def maxima(b, h):
                n = b * PK_HEADS + h
                dve.wait_ge(s_ready, n + 1)
                v.tensor_reduce(negmax[:, 0:1], score_ps[:, 0:P], AX, ALU.max, negate=True)
                step(v.tensor_reduce(negmax[:, 1:2], score_ps[:, P:3 * P], AX, ALU.max, negate=True),
                     max_ready, n + 1)

            def add_output(b, k, h):
                n = b * PK_HEADS + h
                dve.wait_ge(p_ready, n + 1)
                step(v.reciprocal(rrow[:], rowsum[:]))
                settle()
                dve.wait_ge(o_ready, n + 1)
                for t in range(TILES):
                    last = v.scalar_tensor_tensor(acc[k][:, t, :], prob_ps[:, 384 + t * C:384 + (t + 1) * C],
                                                  rrow[:, t:t + 1], acc[k][:, t, :], ALU.mult, ALU.add)
                step(last, acc_ready, n + 1)

            def new_image():
                settle()
                dve.sem_clear(dve_step)
                count[0] = 0

            def image(b, k, left):
                new_image()
                for u in range(UNITS):
                    for what, n in steps(u, left):
                        if what == "weigh" and n not in ON_ACT:
                            unit(b, k, n)
                        if what == "front":
                            front(b + n[0], (k + n[0]) % 2, n[1])
                        if what == "max":
                            maxima(b, n)
                        if what == "add":
                            add_output(b, k, n)

            prepare()
            for s in range(PIECES):
                front(0, 0, s)
                if s == 12:
                    front(1, 1, 0)
                if s == 14:
                    front(1, 1, 1)
            image(0, 0, 2)
            with dve.Fori(0, IMAGES // 2 - 2) as i:
                image(i * 2 + 1, 1, 2)
                image(i * 2 + 2, 0, 2)
            image(IMAGES - 3, 1, 2)
            image(IMAGES - 2, 0, 1)
            image(IMAGES - 1, 1, 0)


def kernel(**inputs):
    import concourse.bacc as _bacc
    from concourse.bass_utils import run_bass_kernel_spmd as _run

    g = {k: np.asarray(v) for k, v in inputs.items()}
    tok = lambda n: g["L0_tok_" + n]
    att = lambda n: g["L0_attn_" + n]
    ffn = lambda n: g["L0_ffn_" + n]
    ident, causal, pos, head = host_constants()
    c = np.ascontiguousarray
    arrays = {
        "x": c(g["x"].reshape(64, 64, 16, 4, 16, 4).transpose(0, 1, 3, 5, 2, 4)).reshape(64, 64, 4096),
        "wkvT": c(tok("Wkv").T),
        "lnkv": c(np.stack([tok("ln_kv_w"), tok("ln_kv_b")], 1)),
        "wqT": c(tok("Wq").T),
        "lnq": c(np.stack([tok("ln_q_w"), tok("ln_q_b")], 1)),
        "projE": c(np.concatenate([tok("proj_w").T, tok("proj_b")[None]], 0)),
        "w_inT": c(att("W_in").T),
        "w_x": c(att("W_xproj")),
        "w_xT": c(att("W_xproj").T),
        "w_dtT": c(att("W_dt").T),
        "b_dt": c(att("b_dt")[:, None]),
        "a_log": c(np.concatenate([att("A_log_f"), att("A_log_b")], 1)),
        "d_skip": c(np.stack([att("D_f"), att("D_b")], 1)),
        "w_global": c(att("W_global")),
        "w_gateT": c(att("W_gate").T),
        "b_global": c(att("b_global").reshape(2, 128).T),
        "b_gate": c(att("b_gate").reshape(2, 128).T),
        "w_outT": c(att("W_out").T),
        "wq_pkT": c(ffn("Wq_pk").reshape(64, 16, 32).transpose(2, 1, 0)).reshape(32, 1024),
        "pk_keysT": c(ffn("pk_keys").transpose(3, 0, 2, 1)).reshape(32, 1024),
        "w_q": c(ffn("Wq")),
        "w_o": c(ffn("Wo")),
        "table": c(np.concatenate([ffn("keys_table"), ffn("values_table")], 1)),
        "ident": ident, "causal": causal, "pos": pos, "headoff": head,
    }
    nc = _bacc.Bacc("TRN2", target_bir_lowering=False, num_devices=1)
    named, args = {}, []
    for name, a in arrays.items():
        named[f"in_{name}_dram"] = a
        args.append(nc.dram_tensor(f"in_{name}_dram", a.shape, mybir.dt.from_np(a.dtype), kind="ExternalInput").ap())
    args.append(nc.dram_tensor("out_dram", (IMAGES, TOK, C), F32, kind="ExternalOutput").ap())
    build(nc, *args)
    r = _run(nc, [named], core_ids=[0])
    return r.results[0]["out_dram"]
```
